# Optimizing a Trainium2 kernel written in Bass

```python
import numpy as np
import jax
import jax.numpy as jnp

def _softmax(x, axis=-1):
    return jax.nn.softmax(x, axis=axis)

def _gelu(x):
    return jax.nn.gelu(x, approximate=True)

def _silu(x):
    return jax.nn.silu(x)

def _sigmoid(x):
    return jax.nn.sigmoid(x)

def _layernorm(x, axis=-1, eps=1e-05):
    m = jnp.mean(x, axis=axis, keepdims=True)
    v = jnp.var(x, axis=axis, keepdims=True)
    return (x - m) / jnp.sqrt(v + eps)

def _scatter_add(tgt, idx, src, axis=0):
    return tgt.at[idx].add(src)

def _segment_sum(src, seg, n):
    return jax.ops.segment_sum(src, seg, n)
kernel_name = 'mk_gnn_preln_d2_gnn_r8_0d15dd'

def setup_inputs(seed: int=0):
    np.random.seed(seed)
    _w = jnp.asarray

    def _rec_inputs():
        import jax
        import jax.numpy as jnp
        _gk = jax.random.key(seed)
        x = -0.0002117 + 1 * jax.random.normal(jax.random.fold_in(_gk, 1), (6250, 512), jnp.float32)
        _s = jax.random.randint(jax.random.fold_in(_gk, 2), (50000,), 0, 6250, jnp.int32)
        _d = jax.random.randint(jax.random.fold_in(_gk, 3), (50000,), 0, 6250, jnp.int32)
        _loop = jnp.arange(6250, dtype=jnp.int32)
        src = jnp.concatenate([_s, _d, _loop])
        dst = jnp.concatenate([_d, _s, _loop])
        _o = jnp.argsort(dst, stable=True)
        src = src[_o]
        dst = dst[_o]
        edge_weight = jax.random.uniform(jax.random.fold_in(_gk, 12), (106250,), jnp.float32, 0.0, 0.999998)
        return (x, src, dst, edge_weight)
    x, src, dst, edge_weight = _rec_inputs()

    def _L0_gnn_setup():
        import jax, jax.numpy as jnp
        import numpy as np
        N_NODES = 6250
        N_EDGES = 100000
        D_IN = 512
        D_OUT = 512
        key = jax.random.key(seed)
        k1, k2, k3, k4, k5 = jax.random.split(key, 5)
        x = jax.random.normal(k1, (N_NODES, D_IN), dtype=jnp.float32)
        weight = jax.random.normal(k2, (D_IN, D_OUT), dtype=jnp.float32) * (1.0 / np.sqrt(D_IN))
        edge_weight = jax.random.uniform(k3, (N_EDGES,), dtype=jnp.float32)
        edge_src = jax.random.randint(k4, (N_EDGES,), 0, N_NODES, dtype=jnp.int32)
        edge_dst = jax.random.randint(k5, (N_EDGES,), 0, N_NODES, dtype=jnp.int32)
        return {'x': x, 'weight': weight, 'edge_weight': edge_weight, 'edge_src': edge_src, 'edge_dst': edge_dst}
    _L0_gnn_all = _L0_gnn_setup()
    _L0_gnn_in = {k: v for k, v in _L0_gnn_all.items() if k in ('weight',)}
    del _L0_gnn_all

    def _L1_gnn_setup():
        import jax, jax.numpy as jnp
        import numpy as np
        N_NODES = 6250
        D = 512
        N_EDGES = 200000
        key = jax.random.key(seed)
        ks = jax.random.split(key, 5)
        x = jax.random.normal(ks[0], (N_NODES, D), dtype=jnp.float32)
        W = jax.random.normal(ks[1], (D, D), dtype=jnp.float32) * (1.0 / np.sqrt(D))
        b = jnp.zeros((D,), dtype=jnp.float32)
        edge_weight = jax.random.uniform(ks[2], (N_EDGES,), dtype=jnp.float32)
        edge_src = jax.random.randint(ks[3], (N_EDGES,), 0, N_NODES, dtype=jnp.int32)
        edge_dst = jax.random.randint(ks[4], (N_EDGES,), 0, N_NODES, dtype=jnp.int32)
        return {'x': x, 'W': W, 'b': b, 'edge_weight': edge_weight, 'edge_src': edge_src, 'edge_dst': edge_dst}
    _L1_gnn_all = _L1_gnn_setup()
    _L1_gnn_in = {k: v for k, v in _L1_gnn_all.items() if k in ('W', 'b')}
    del _L1_gnn_all
    return {'x': x, 'src': src, 'dst': dst, 'edge_weight': edge_weight, 'L0_gnn_weight': _L0_gnn_in['weight'], 'L1_gnn_W': _L1_gnn_in['W'], 'L1_gnn_b': _L1_gnn_in['b']}

def reference(x, src, dst, edge_weight, L0_gnn_weight, L1_gnn_W, L1_gnn_b):
    import jax
    import jax.numpy as jnp

    def _L0_gnn_ref(x, weight, edge_weight, edge_src, edge_dst):
        import jax, jax.numpy as jnp
        import numpy as np
        N_NODES = 6250
        N_EDGES = 100000
        D_IN = 512
        D_OUT = 512
        support = jnp.matmul(x, weight)
        msgs = support[edge_src] * edge_weight[:, None]
        output = jax.ops.segment_sum(msgs, edge_dst, num_segments=N_NODES)
        return output

    def _L1_gnn_ref(x, W, b, edge_weight, edge_src, edge_dst):
        import jax, jax.numpy as jnp
        import numpy as np
        N_NODES = 6250
        D = 512
        N_EDGES = 200000
        support = x @ W
        msgs = support[edge_src] * edge_weight[:, None]
        agg = jax.ops.segment_sum(msgs, edge_dst, num_segments=x.shape[0])
        gc_out = agg + b
        return jax.nn.relu(gc_out) + x
    h = jnp.maximum(_layernorm(x, axis=-1), 0.0)
    x = x + _L0_gnn_ref(h, L0_gnn_weight, edge_weight, src, dst)
    h = jnp.maximum(_layernorm(x, axis=-1), 0.0)
    x = x + _L1_gnn_ref(h, L1_gnn_W, L1_gnn_b, edge_weight, src, dst)
    return x

_drawn_inputs = setup_inputs


def setup_inputs(seed=0):
    import zlib

    import numpy as np

    out = dict(_drawn_inputs(seed))
    spreads = {'L1_gnn_b': (0.0, 0.708)}
    factors = {}
    for name, (base, spread) in spreads.items():
        noise = np.random.default_rng([zlib.crc32(name.encode()), seed]).standard_normal(out[name].shape)
        drawn = base * np.exp(spread * noise) if base else spread * noise
        out[name] = jnp.asarray(drawn.astype(out[name].dtype))
    for name, factor in factors.items():
        out[name] = (out[name] * factor).astype(out[name].dtype)
    return out
```

```python
import numpy as np
import concourse.bass as bass
from concourse import mybir
from contextlib import ExitStack


def gnn_kernel(nc, x, src, dst, edge_weight, w_first, w_second, bias, out):
    f32, bf16, f16, i32 = mybir.dt.float32, mybir.dt.bfloat16, mybir.dt.float16, mybir.dt.int32
    ALU = mybir.AluOpType
    ACT = mybir.ActivationFunctionType
    AX = mybir.AxisListType

    P = 128
    N, D = x.shape
    E = src.shape[0]
    KD = D // P
    TILES = -(-N // P)
    REST = N - (TILES - 1) * P
    REAL = -(-E // P)
    GC, GB = 4, 4
    BLOCK = GC * GB
    BLOCKS = 2 * -(-REAL // (2 * BLOCK))
    CHUNKS = BLOCKS * BLOCK
    GROUPS = BLOCKS * GB
    PADS = CHUNKS * P - E
    NAT = -(-REAL // P)
    WIN = 42
    LAG = 6
    LATE = TILES - (BLOCKS - LAG)
    COLS = TILES * P + WIN
    NOWHERE = float(1 << 20)
    SCALE = 2048.0
    EPS = 1e-5
    START = 8
    AHEAD = 3
    LN = 3
    STEPS = (TILES - 1) // LN
    assert STEPS % 2 == 0 and STEPS * LN == TILES - 1 and LATE == 3 and BLOCKS % 2 == 0 and LAG % 2 == 0

    ctx = ExitStack()
    with ctx:
        def sb(name, shape, dt):
            return ctx.enter_context(nc.sbuf_tensor(name, shape, dt))

        def sem(name):
            return ctx.enter_context(nc.semaphore(name))

        h_dram = [nc.dram_tensor(f"h{l}_dram", (N, 2 * D), f16, kind="Internal").ap() for l in range(2)]
        y_dram = nc.dram_tensor("y_dram", (N, D), f32, kind="Internal").ap()
        sum_dram = nc.dram_tensor("sum_dram", (N + P, D), f32, kind="Internal").ap()

        aggT = sb("aggT", [P, KD, COLS], f32)
        rows = sb("rows", [P, BLOCK, 2 * D], f16)
        idxT = sb("idxT", [P, CHUNKS + BLOCK], i32)
        dstT = sb("dstT", [P, CHUNKS], f32)
        wT = sb("wT", [P, CHUNKS], f32)
        relT = sb("relT", [P, CHUNKS + AHEAD * GC], bf16)
        w3 = sb("w3", [P, CHUNKS + AHEAD * GC, 3], bf16)
        idx_now = sb("idx_now", [P, 2, BLOCK], i32)
        wmat = sb("wmat", [P, 2, KD, D], f32)
        ident = sb("ident", [P, P], f32)
        fold = sb("fold", [P, WIN], f32)
        row0 = sb("row0", [P, P], f32)
        iota_w = sb("iota_w", [P, WIN], bf16)
        ones = sb("ones", [P, 1], f32)
        zero = sb("zero", [P, 1], f32)
        eps = sb("eps", [P, 1], f32)
        low = sb("low", [1, GROUPS], f32)
        base_i = sb("base_i", [1, GROUPS], i32)
        early = sb("early", [1, GROUPS], f32)
        counts = sb("counts", [P, 3], f32)
        flag_f = sb("flag_f", [1, 2], f32)
        flag_i = sb("flag_i", [1, 1], i32)
        stats = sb("stats", [P, 2, LN, 6], f32)
        mv = sb("mv", [P, 2, LN, 2], f32)
        std = sb("std", [P, 2, LN], f32)
        rstd = sb("rstd", [P, 2, LN], f32)
        shift = sb("shift", [P, 2, LN], f32)
        scratch = sb("scratch", [P, 3 * 2 * LN * D], f32)

        z = 2 * LN * D
        ln_x = scratch[:, 0:z].rearrange("p (b t d) -> p b t d", b=2, t=LN)
        ln_h = scratch[:, z:2 * z].rearrange("p (b t d) -> p b t d", b=2, t=LN)
        ln_pair = scratch[:, 2 * z:3 * z].bitcast(f16).rearrange("p (b t d) -> p b t d", b=2, t=LN)
        at = [0]

        def part(words):
            at[0] += words
            assert at[0] <= 3 * z
            return scratch[:, at[0] - words:at[0]]

        xt = part(2 * D).rearrange("p (b d) -> p b d", b=2)
        ht = part(2 * D).rearrange("p (b d) -> p b d", b=2)
        pair_words = part(2 * D)
        pair = pair_words.bitcast(f16).rearrange("p (b d) -> p b d", b=2)
        out_t = pair_words.rearrange("p (b d) -> p b d", b=2)
        stage = part(2 * D).rearrange("p (b k n) -> p b k n", b=2, k=KD)
        agg = part(2 * D).rearrange("p (b d) -> p b d", b=2)
        hot3 = part(4 * GC * P // 2).bitcast(bf16).rearrange("p (b c m) -> p b c m", b=4, c=GC)
        hot = part(2 * GC * WIN // 2).bitcast(bf16).rearrange("p (b c j) -> p b c j", b=2, c=GC)
        bias_t = part(D)
        dst_b, eq, eqw, below = (part(P) for _ in range(4))
        col = part(8)
        trash = part(1)
        gen_idx, gen_to = (part(1).bitcast(i32) for _ in range(2))

        temp = rows[:, :, :].rearrange("p a b -> p (a b)").bitcast(f32)
        w_nat = NAT * P

        def table(k):
            return temp[:, k * w_nat:(k + 1) * w_nat].rearrange("p (g e) -> p g e", g=NAT)

        src_nat, dst_nat = table(0).bitcast(i32), table(1).bitcast(i32)
        nat_f = [table(2), table(3), table(4)]
        rel_f = temp[:, 5 * w_nat:5 * w_nat + CHUNKS]
        rem = temp[:, 6 * w_nat:6 * w_nat + CHUNKS]
        junk = temp[:, 7 * w_nat:7 * w_nat + CHUNKS]

        ps = ctx.enter_context(nc.psum_tensor("ps", [P, 8, D], f32))
        turned = [ps[:, 2 * k:2 * k + 2, :].rearrange("p a b -> p (a b)") for k in range(3)]

        s_const = sem("constants_made")
        s_fill = sem("tables_filled")
        s_tab = sem("edge_tables_loaded")
        s_conv = sem("tables_as_float")
        s_turn = sem("tables_turned")
        s_dstT = sem("dst_table_ready")
        s_base = sem("bases_spread")
        s_cnt = sem("counts_ready")
        s_tot = sem("totals_ready")
        s_flag = sem("flag_ready")
        s_link = sem("vector_chain")
        s_wld = sem("weights_loaded")
        s_zero = sem("sums_zeroed")
        s_lnx = [sem(f"ln_x_loaded{b}") for b in range(2)]
        s_lnst = [sem(f"ln_pair_stored{b}") for b in range(2)]
        s_lnmv = sem("ln_moments")
        s_lnsd = sem("ln_std")
        s_lnsh = sem("ln_shift")
        s_lnh = sem("ln_h")
        s_lnlo = sem("ln_remainder")
        s_index_go = sem("pool_may_gather")
        s_aggr_go = sem("vector_may_aggregate")
        s_idx = sem("indices_staged")
        s_rows = [sem(f"rows_gathered{b}") for b in range(GB)]
        s_hot = sem("onehot_made")
        s_hot3 = sem("weights_in_place")
        s_sum = sem("group_summed")
        s_evac = sem("sum_copied")
        s_fold = sem("group_folded")
        s_add = sem("group_added")
        s_stage = sem("tile_staged")
        s_clear = sem("tile_cleared")
        s_proj = sem("tile_projected")
        s_x1 = sem("residual_added")
        s_mv = sem("tile_moments")
        s_std = sem("tile_std")
        s_shift = sem("tile_shift")
        s_h = sem("tile_h")
        s_pair = sem("tile_pair")
        s_out = sem("tile_out")
        s_ld = [[sem(f"tile_loaded{l}{b}") for b in range(2)] for l in range(2)]
        s_hst = [sem(f"h_stored{b}") for b in range(2)]
        s_yst = [sem(f"y_stored{b}") for b in range(2)]
        s_ost = [sem(f"out_stored{b}") for b in range(2)]
        g_link = sem("g_vector_chain")
        g_zero = sem("g_zero_tile")
        g_ones = sem("g_ones_made")
        g_zst = sem("g_sums_cleared")
        g_idx = sem("g_index_copied")
        g_rows = sem("g_rows_gathered")
        g_dstb = sem("g_dst_spread")
        g_row = sem("g_dst_row")
        g_eq = sem("g_matrix_ready")
        g_sum = sem("g_chunk_summed")
        g_msg = sem("g_chunk_copied")
        g_sc = sem("g_chunk_added")
        g_ld = sem("g_tile_loaded")
        g_tr = sem("g_tile_turned")

        block = ctx.enter_context(nc.Block())
        wm = [w_first, w_second]

        def whole(t):
            return t * P, (REST if isinstance(t, int) and t == TILES - 1 else P)

        def node_rows(ap, t):
            n0, n = whole(t)
            return ap[bass.ds(n0, n), :]

        @block.sync
        def _(sp):
            xg = x[0:STEPS * LN * P, :].rearrange("(s t p) d -> s p t d", t=LN, p=P)
            hg = h_dram[0][0:STEPS * LN * P, :].rearrange("(s t p) d -> s p t d", t=LN, p=P)

            def ln_store(step, b, n):
                sp.wait_ge(s_lnlo, n)
                sp.dma_start(hg[step] if isinstance(step, int) else
                             hg[bass.ds(step, 1)].rearrange("s p t d -> (s p) t d"),
                             ln_pair[:, b]).then_inc(s_lnst[b], 16)

            def ln_load(step, b):
                sp.dma_start(ln_x[:, b], xg[step] if isinstance(step, int) else
                             xg[bass.ds(step, 1)].rearrange("s p t d -> (s p) t d")).then_inc(s_lnx[b], 16)

            ln_load(0, 0)
            ln_load(1, 1)
            with sp.Fori(0, STEPS // 2 - 1) as j:
                for b in range(2):
                    sp.wait_ge(s_lnh, 2 * j + b + 1)
                    ln_load(2 * j + b + 2, b)
                    ln_store(2 * j + b, b, 2 * j + b + 1)
            sp.wait_ge(s_lnh, STEPS - 1)
            sp.dma_start(ln_x[0:REST, 0, 0, :], x[N - REST:N, :]).then_inc(s_lnx[0], 16)
            ln_store(STEPS - 2, 0, STEPS - 1)
            ln_store(STEPS - 1, 1, STEPS)
            sp.wait_ge(s_lnlo, STEPS + 1)
            sp.dma_start(h_dram[0][N - REST:N, :], ln_pair[0:REST, 0, 0, :]).then_inc(s_lnst[0], 16)
            sp.wait_ge(s_lnst[0], 16 * (STEPS // 2 + 1))
            sp.wait_ge(s_lnst[1], 16 * (STEPS // 2))

            def load(l, t, b):
                n0, n = whole(t)
                sp.dma_start(xt[0:n, b, :], node_rows(x if l == 0 else y_dram, t)).then_inc(s_ld[l][b], 16)

            def store_first(t, b, k):
                n0, n = whole(t)
                sp.wait_ge(s_pair, START + t + 1)
                sp.dma_start(node_rows(h_dram[1], t), pair[0:n, b, :]).then_inc(s_hst[b], 16)
                sp.dma_start(node_rows(y_dram, t), xt[0:n, b, :]).then_inc(s_yst[b], 16)
                sp.wait_ge(s_yst[b], 16 * k)

            def store_second(t, b):
                n0, n = whole(t)
                sp.wait_ge(s_out, t + 1)
                sp.dma_start(node_rows(out, t), out_t[0:n, b, :]).then_inc(s_ost[b], 16)

            for l in range(2):
                load(l, 0, 0)
                load(l, 1, 1)
                if l == 0:
                    sp.dma_start(bias_t, bias.rearrange("(a d) -> a d", a=1).to_broadcast([P, D])).then_inc(s_wld, 16)
                with sp.Fori(0, TILES // 2 - 1) as j:
                    for b in range(2):
                        if l == 0:
                            store_first(2 * j + b, b, j + 1)
                        else:
                            store_second(2 * j + b, b)
                        load(l, 2 * j + b + 2, b)
                for t in range(TILES - 3, TILES):
                    b = t % 2
                    if l == 0:
                        store_first(t, b, t // 2 + 1)
                    else:
                        store_second(t, b)
                    if t == TILES - 3:
                        load(l, TILES - 1, 0)
                for b in range(2):
                    total = 16 * (TILES // 2 + 1 - b)
                    if l == 0:
                        sp.wait_ge(s_hst[b], total)
                        sp.wait_ge(s_yst[b], total)
                    else:
                        sp.wait_ge(s_ost[b], total)

        @block.gpsimd
        def _(pool):
            nc.gpsimd.memset(ident[:, :], 0.0).then_inc(s_const, 1)
            nc.gpsimd.memset(fold[:, :], 0.0).then_inc(s_const, 1)
            nc.gpsimd.memset(row0[:, :], 0.0).then_inc(s_const, 1)
            pool.wait_ge(s_const, 3)
            nc.gpsimd.affine_select(out=ident[:, :], in_=ident[:, :], compare_op=ALU.not_equal, fill=1.0,
                                    base=0, pattern=[[-1, P]], channel_multiplier=1).then_inc(s_const, 1)
            for k in range(3):
                nc.gpsimd.affine_select(out=fold[:, :], in_=fold[:, :], compare_op=ALU.not_equal,
                                        fill=1.0 / SCALE, base=-k * WIN, pattern=[[-1, WIN]],
                                        channel_multiplier=1).then_inc(s_const, 1)
                pool.wait_ge(s_const, 5 + k)
            nc.gpsimd.affine_select(out=row0[:, :], in_=row0[:, :], compare_op=ALU.not_equal, fill=1.0,
                                    base=0, pattern=[[0, P]], channel_multiplier=1).then_inc(s_const, 1)
            nc.gpsimd.iota(iota_w[:, :], pattern=[[1, WIN]], base=0, channel_multiplier=0,
                           allow_small_or_imprecise_dtypes=True).then_inc(s_const, 1)
            nc.gpsimd.iota(low[:, :], pattern=[[P, BLOCKS], [0, GB]], base=-(LAG - 2) * P, channel_multiplier=0,
                           allow_small_or_imprecise_dtypes=True).then_inc(s_const, 1)
            nc.gpsimd.memset(aggT[:, :, :], 0.0).then_inc(s_zero, 1)

            pool.wait_ge(s_flag, 1)
            flag = pool.value_load(flag_i[0:1, 0:1], min_val=0, max_val=1)

            def h_ready(l):
                for b in range(2):
                    if l == 0:
                        pool.wait_ge(s_lnst[b], 16 * (STEPS // 2 + 1 - b))
                    else:
                        pool.wait_ge(s_hst[b], 16 * (TILES // 2 + 1 - b))

            def before_indexed():
                pool.sem_inc(s_index_go, 1)

            with pool.If(flag == 1):
                for l in range(2):
                    if l == 1:
                        pool.wait_ge(s_idx, BLOCKS + 1)
                    nc.gpsimd.tensor_copy(idx_now[:, 0, :], idxT[:, 0:BLOCK]).then_inc(s_idx, 1)
                    h_ready(l)
                    with pool.Fori(0, BLOCKS // 2) as i:
                        for m in range(2):
                            bl = 2 * i + m
                            pool.wait_ge(s_idx, l * (BLOCKS + 1) + bl + 1)
                            for q in range(GB):
                                g = l * GROUPS + bl * GB + q
                                pool.wait_ge(s_sum, START + g + 1 - GB)
                                if q == GB - 1:
                                    nc.gpsimd.tensor_copy(idx_now[:, 1 - m, :], idxT[:, bass.ds((bl + 1) * BLOCK, BLOCK)]
                                                          ).then_inc(s_idx, 1)
                                before_indexed()
                                for c in range(GC):
                                    k = q * GC + c
                                    pool.indirect_dma_start(
                                        out=rows[:, k, :], out_offset=None, in_=h_dram[l][:, :],
                                        in_offset=bass.IndirectOffsetOnAxis(ap=idx_now[:, m, k:k + 1], axis=0),
                                    ).then_inc(s_rows[q], 16)
            with pool.Else():
                for l in range(2):
                    h_ready(l)
                    if l == 1:
                        pool.wait_ge(g_ld, 16 * TILES)
                    nc.gpsimd.memset(agg[:, 0, :], 0.0).then_inc(g_zero, 1)
                    nc.gpsimd.memset(below, 1.0).then_inc(g_ones, 1)
                    pool.wait_ge(g_ones, l + 1)
                    nc.gpsimd.affine_select(out=below, in_=below, compare_op=ALU.is_gt, fill=0.0, base=0,
                                            pattern=[[-1, P]], channel_multiplier=1).then_inc(g_zero, 1)
                    nc.gpsimd.iota(trash, pattern=[[0, 1]], base=N, channel_multiplier=1,
                                   allow_small_or_imprecise_dtypes=True).then_inc(g_zero, 1)
                    pool.wait_ge(g_zero, 3 * l + 3)
                    with pool.Fori(0, TILES) as t:
                        pool.dma_start(sum_dram[bass.ds(t * P, P), :], agg[:, 0, :]).then_inc(g_zst, 16)
                    pool.dma_start(sum_dram[TILES * P:N + P, :], agg[0:N + P - TILES * P, 0, :]).then_inc(g_zst, 16)
                    pool.wait_ge(g_zst, 16 * (TILES + 1) * (l + 1))
                    with pool.Fori(0, CHUNKS) as c:
                        n = l * CHUNKS + c
                        nc.gpsimd.tensor_copy(gen_idx, idxT[:, bass.ds(c, 1)]).then_inc(g_idx, 1)
                        pool.wait_ge(g_idx, n + 1)
                        before_indexed()
                        pool.indirect_dma_start(
                            out=rows[:, 0, :], out_offset=None, in_=h_dram[l][:, :],
                            in_offset=bass.IndirectOffsetOnAxis(ap=gen_idx, axis=0)).then_inc(g_rows, 16)
                        pool.wait_ge(g_msg, n + 1)
                        before_indexed()
                        pool.indirect_dma_start(
                            out=sum_dram[:, :], out_offset=bass.IndirectOffsetOnAxis(ap=gen_to, axis=0),
                            in_=agg[:, 1, :], in_offset=None, compute_op=ALU.add).then_inc(g_sc, 16)
                        pool.wait_ge(g_sc, 16 * n + 16)

        @block.scalar
        def _(act):
            act.wait_ge(s_fill, 1)
            full = (NAT - 1) * P * P
            more = (E - full) // P
            for nat, edges in ((dst_nat, dst), (src_nat, src), (nat_f[2], edge_weight)):
                act.dma_start(nat[:, 0:NAT - 1, :], edges[0:full].rearrange("(g p e) -> p g e", p=P, e=P)
                              ).then_inc(s_tab, 16)
                act.dma_start(nat[0:more, NAT - 1, :], edges[full:full + more * P].rearrange("(p e) -> p e", e=P)
                              ).then_inc(s_tab, 16)
                act.dma_start(nat[more:more + 1, NAT - 1, 0:E - full - more * P],
                              edges[full + more * P:E].rearrange("(p e) -> p e", p=1)).then_inc(s_tab, 16)
            for l in range(2):
                act.dma_start(wmat[:, l], wm[l].rearrange("(k p) d -> p k d", p=P)).then_inc(s_wld, 16)

            def ln_std(b, n, t=LN):
                act.wait_ge(s_lnmv, n)
                act.activation(std[:, b, 0:t], mv[:, b, 0:t, 1], ACT.Sqrt, bias=eps[:, :],
                               scale=1.0 / SCALE ** 2).then_inc(s_lnsd, 1)

            def ln_relu(b, n, t=LN, stored=None):
                act.wait_ge(s_lnsh, n)
                if stored is not None:
                    act.wait_ge(s_lnst[b], stored)
                for k in range(t):
                    for o in (ln_h, ln_pair):
                        last = act.activation(o[:, b, k, 0:D], ln_x[:, b, k, :], ACT.Relu,
                                              bias=shift[:, b, k:k + 1], scale=rstd[:, b, k:k + 1])
                last.then_inc(s_lnh, 1)

            act.wait_ge(s_const, 10)
            for b in range(2):
                ln_std(b, b + 1)
            for b in range(2):
                ln_relu(b, b + 1)
            with act.Fori(1, STEPS // 2) as j:
                for b in range(2):
                    ln_std(b, 2 * j + b + 1)
                for b in range(2):
                    ln_relu(b, 2 * j + b + 1, stored=16 * j)
            ln_std(0, STEPS + 1, 1)
            ln_relu(0, STEPS + 1, 1, 16 * (STEPS // 2))

            act.wait_ge(s_flag, 1)
            flag = act.value_load(flag_i[0:1, 0:1], min_val=0, max_val=1)

            def stage_tile(n, b, t, added):
                act.wait_ge(s_add, added)
                act.wait_ge(s_proj, START + n - 1)
                act.activation(stage[:, b], aggT[:, :, bass.ds(t * P, P)], ACT.Copy).then_inc(s_stage, 1)

            def std_tile(n, b):
                act.wait_ge(s_mv, n + 1)
                act.activation(std[:, b, 0:1], mv[:, b, 0, 1:2], ACT.Sqrt, bias=eps[:, :],
                               scale=1.0 / SCALE ** 2).then_inc(s_std, 1)

            def relu_tile(n, b, stored):
                act.wait_ge(s_shift, n + 1)
                act.wait_ge(s_pair, START + n - 1)
                if stored is not None:
                    act.wait_ge(s_hst[b], stored)
                act.activation(ht[:, b, :], xt[:, b, :], ACT.Relu, bias=shift[:, b, 0:1], scale=rstd[:, b, 0:1])
                act.activation(pair[:, b, 0:D], xt[:, b, :], ACT.Relu, bias=shift[:, b, 0:1],
                               scale=rstd[:, b, 0:1]).then_inc(s_h, 1)

            act.sem_inc(s_evac, START)
            with act.If(flag == 1):
                for l in range(2):
                    def body(i, take, first):
                        for m in range(2):
                            bl = 2 * i + m
                            t = bl - LAG
                            n = l * TILES + t
                            if take:
                                stage_tile(n, m, t, START + l * GROUPS + GB * (bl - 1))
                            for q in range(GB):
                                g = l * GROUPS + bl * GB + q
                                act.wait_ge(s_sum, START + g + 1)
                                act.wait_ge(s_fold, START + g - 1)
                                act.activation(agg[:, q % 2, :], ps[:, q, :], ACT.Copy).then_inc(s_evac, 1)
                                if take and l == 0 and q == 1:
                                    std_tile(n, m)
                                if take and l == 0 and q == 2:
                                    relu_tile(n, m, None if first else 16 * (i - LAG // 2))

                    with act.Fori(0, LAG // 2) as i:
                        body(i, False, False)
                    body(LAG // 2, True, True)
                    with act.Fori(LAG // 2 + 1, BLOCKS // 2) as i:
                        body(i, True, False)
                    for t in range(TILES - LATE, TILES):
                        n, b = l * TILES + t, t % 2
                        stage_tile(n, b, t, START + (l + 1) * GROUPS)
                        if l == 0:
                            std_tile(n, b)
                            relu_tile(n, b, 16 * (t // 2))
            with act.Else():
                for l in range(2):
                    with act.Fori(0, CHUNKS) as c:
                        n = l * CHUNKS + c
                        act.wait_ge(g_sum, n + 1)
                        act.activation(agg[:, 1, :], ps[:, 0, :], ACT.Copy, scale=1.0 / SCALE).then_inc(g_msg, 1)

                    def gen_tile(t, b, stored):
                        n = l * TILES + t
                        act.dma_start(agg[:, 0, :], sum_dram[bass.ds(t * P, P), :]).then_inc(g_ld, 16)
                        act.wait_ge(g_tr, n + 1)
                        act.wait_ge(s_proj, START + n - 1)
                        act.activation(stage[:, b], ps[:, 4, :].rearrange("p (k n) -> p k n", k=KD), ACT.Copy
                                       ).then_inc(s_stage, 1)
                        if l == 0:
                            std_tile(n, b)
                            relu_tile(n, b, stored)

                    act.wait_ge(g_sc, 16 * CHUNKS * (l + 1))
                    for b in range(2):
                        gen_tile(b, b, None)
                    with act.Fori(1, TILES // 2) as j:
                        for b in range(2):
                            gen_tile(2 * j + b, b, 16 * j)
                    gen_tile(TILES - 1, 0, 16 * (TILES // 2))

        @block.tensor
        def _(pe):
            pe.wait_ge(s_const, 4)
            for k, name in ((1, "dst"), (0, "src"), (2, "weight")):
                if name == "weight":
                    pe.wait_ge(s_tab, 9 * 16)
                else:
                    pe.wait_ge(s_conv, 1 + (k == 0))
                for g in range(NAT):
                    last = nc.tensor.transpose(turned[k][:, g * P:(g + 1) * P], nat_f[k][:, g, :], ident[:, :])
                last.then_inc(s_turn, 1)
            pe.wait_ge(s_const, 8)
            pe.wait_ge(s_dstT, 1)
            nc.tensor.matmul(ps[:, 6, 0:GROUPS], row0[:, :], dstT[:, ::GC], start=True, stop=True).then_inc(s_base, 1)
            pe.wait_ge(s_cnt, 1)
            nc.tensor.matmul(ps[0:1, 7, 0:3], ones[:, :], counts[:, :], start=True, stop=True).then_inc(s_tot, 1)
            pe.wait_ge(s_wld, 48)

            pe.wait_ge(s_flag, 1)
            flag = pe.value_load(flag_i[0:1, 0:1], min_val=0, max_val=1)
            pe.sem_inc(s_sum, START)
            pe.sem_inc(s_fold, START)
            pe.sem_inc(s_proj, START)

            def project(l, n, b):
                pe.wait_ge(s_stage, n + 1)
                pe.wait_ge(s_x1, START + n - 1)
                for k in range(KD):
                    last = nc.tensor.matmul(ps[:, 6 + b, :], stage[:, b, k, :], wmat[:, l, k, :],
                                            start=(k == 0), stop=(k == KD - 1))
                last.then_inc(s_proj, 1)

            with pe.If(flag == 1):
                for l in range(2):
                    def add_up(bl, q):
                        g = l * GROUPS + bl * GB + q
                        pe.wait_ge(s_rows[q], 16 * GC * (l * BLOCKS + bl + 1))
                        pe.wait_ge(s_hot3, START + g + 1)
                        pe.wait_ge(s_evac, START + g + 1 - GB)
                        for c in range(GC):
                            for part_ in range(2):
                                last = nc.tensor.matmul(
                                    ps[:, q, :], hot3[:, q, c, :],
                                    rows[:, q * GC + c, part_ * D:(part_ + 1) * D],
                                    start=(c == 0 and part_ == 0), stop=(c == GC - 1 and part_ == 1))
                        last.then_inc(s_sum, 1)

                    def fold_up(bl, q):
                        g = l * GROUPS + bl * GB + q
                        pe.wait_ge(s_evac, START + g + 1)
                        pe.wait_ge(s_add, START + g - 1)
                        for k in range(KD):
                            last = nc.tensor.matmul(ps[:, 4 + q % 2, k * WIN:(k + 1) * WIN],
                                                    agg[:, q % 2, k * P:(k + 1) * P], fold[:, :],
                                                    start=True, stop=True)
                        last.then_inc(s_fold, 1)

                    def body(i, take):
                        for m in range(2):
                            bl = 2 * i + m
                            for q in range(GB):
                                add_up(bl, q)
                                if take and q == 1:
                                    project(l, l * TILES + bl - LAG, m)
                                if q or m:
                                    fold_up(bl if q else bl - 1, (q - 1) % GB)
                        fold_up(2 * i + 1, GB - 1)

                    with pe.Fori(0, LAG // 2) as i:
                        body(i, False)
                    with pe.Fori(LAG // 2, BLOCKS // 2) as i:
                        body(i, True)
                    for t in range(TILES - LATE, TILES):
                        project(l, l * TILES + t, t % 2)
            with pe.Else():
                for l in range(2):
                    with pe.Fori(0, CHUNKS) as c:
                        n = l * CHUNKS + c
                        pe.wait_ge(g_dstb, n + 1)
                        nc.tensor.matmul(ps[:, 1, 0:P], dst_b, ident[:, :], start=True, stop=True).then_inc(g_row, 1)
                        pe.wait_ge(g_eq, n + 1)
                        nc.tensor.matmul(ps[:, 0, :], eqw, ht[:, 0, :], start=True, stop=True).then_inc(g_sum, 1)

                    def gen_tile(t, b):
                        n = l * TILES + t
                        pe.wait_ge(g_ld, 16 * (n + 1))
                        for k in range(KD):
                            last = nc.tensor.transpose(ps[:, 4, k * P:(k + 1) * P], agg[:, 0, k * P:(k + 1) * P],
                                                       ident[:, :])
                        last.then_inc(g_tr, 1)
                        project(l, n, b)

                    with pe.Fori(0, TILES // 2) as j:
                        for b in range(2):
                            gen_tile(2 * j + b, b)
                    gen_tile(TILES - 1, 0)

        @block.vector
        def _(dve):
            nc.vector.memset(src_nat[:, NAT - 1, :], 0)
            nc.vector.memset(dst_nat[:, NAT - 1, :], int(NOWHERE))
            nc.vector.memset(nat_f[2][:, NAT - 1, :], 0.0).then_inc(s_fill, 1)
            nc.vector.memset(idxT[:, :], 0)
            nc.vector.memset(counts[:, :], 0.0)
            nc.vector.memset(ones[:, :], 1.0)
            nc.vector.memset(zero[:, :], 0.0)
            nc.vector.memset(eps[:, :], EPS / SCALE ** 2)
            nc.vector.memset(ln_x[:, :, :, :], 0.0).then_inc(s_const, 0 + 0) if False else None
            chain = [0]

            def link(ins):
                chain[0] += 1
                ins.then_inc(s_link, 1)
                dve.wait_ge(s_link, chain[0])

            link(nc.vector.memset(junk, 0.0))
            dve.wait_ge(s_tab, 9 * 16)
            nc.vector.tensor_copy(nat_f[1], dst_nat).then_inc(s_conv, 1)
            nc.vector.tensor_copy(nat_f[0], src_nat).then_inc(s_conv, 1)
            dve.wait_ge(s_turn, 1)
            nc.vector.tensor_copy(dstT[:, :], turned[1][:, 0:CHUNKS]).then_inc(s_dstT, 1)
            dve.wait_ge(s_turn, 3)
            nc.vector.tensor_copy(idxT[:, 0:CHUNKS], turned[0][:, 0:CHUNKS])
            link(nc.vector.tensor_copy(wT[:, :], turned[2][:, 0:CHUNKS]))
            link(nc.vector.tensor_copy(w3[:, 0:CHUNKS, 0], wT[:, :]))
            link(nc.vector.tensor_tensor(rem, wT[:, :], w3[:, 0:CHUNKS, 0], ALU.subtract))
            link(nc.vector.tensor_copy(w3[:, 0:CHUNKS, 1], rem))
            link(nc.vector.tensor_tensor(rem, rem, w3[:, 0:CHUNKS, 1], ALU.subtract))
            link(nc.vector.tensor_copy(w3[:, 0:CHUNKS, 2], rem))
            dve.wait_ge(s_base, 1)
            link(nc.vector.tensor_tensor(rel_f.rearrange("p (g c) -> p g c", c=GC),
                                         dstT[:, :].rearrange("p (g c) -> p g c", c=GC),
                                         ps[:, 6, 0:GROUPS].unsqueeze(2).to_broadcast([P, GROUPS, GC]),
                                         ALU.subtract))
            link(nc.vector.tensor_copy(relT[:, 0:CHUNKS], rel_f))
            nc.vector.tensor_copy(relT[:, CHUNKS:CHUNKS + AHEAD * GC], relT[:, 0:AHEAD * GC])
            nc.vector.tensor_copy(w3[:, CHUNKS:CHUNKS + AHEAD * GC, :], w3[:, 0:AHEAD * GC, :])
            nc.vector.tensor_copy(base_i[:, :], ps[0:1, 6, 0:GROUPS])
            link(nc.vector.tensor_scalar(junk, rel_f, float(WIN), 0.0, ALU.is_ge, ALU.add, accum_out=counts[:, 0:1]))
            link(nc.vector.tensor_scalar(junk, rel_f, 0.0, 0.0, ALU.is_lt, ALU.add, accum_out=counts[:, 1:2]))
            dve.wait_ge(s_const, 10)
            link(nc.vector.tensor_tensor(early[:, :], ps[0:1, 6, 0:GROUPS], low[:, :], ALU.is_lt))
            nc.vector.tensor_reduce(counts[0:1, 2:3], early[:, :], AX.X, ALU.add).then_inc(s_cnt, 1)
            dve.wait_ge(s_tot, 1)
            link(nc.vector.tensor_scalar(flag_f[:, 1:2], ps[0:1, 7, 2:3], float(P * CHUNKS), None, ALU.mult))
            link(nc.vector.tensor_scalar(flag_f[:, 0:1], ps[0:1, 7, 0:1], flag_f[:, 1:2], None, ALU.add))
            link(nc.vector.tensor_scalar(flag_f[:, 1:2], flag_f[:, 0:1], ps[0:1, 7, 1:2], float(PADS), ALU.add, ALU.is_equal))
            nc.vector.tensor_copy(flag_i[:, :], flag_f[:, 1:2]).then_inc(s_flag, 1)

            def ln_stats(b, n, loaded, t=LN, p=P):
                dve.wait_ge(s_lnx[b], loaded)
                for k in range(t):
                    last = nc.vector.bn_stats(stats[0:p, b, k, :], ln_x[0:p, b, k, :])
                last.then_inc(s_x1, 1)
                return n

            ln_n = [0]

            def ln_moments(b, n, loaded, t=LN):
                dve.wait_ge(s_lnx[b], loaded)
                for k in range(t):
                    last = nc.vector.bn_stats(stats[:, b, k, :], ln_x[:, b, k, :])
                last.then_inc(s_clear, 1)
                dve.wait_ge(s_clear, n)
                dve.sem_inc(s_aggr_go, 1)
                for k in range(t):
                    last = nc.vector.bn_aggr(mv[:, b, k, :], stats[:, b, k, :])
                last.then_inc(s_lnmv, 1)

            def ln_shift(b, n, t=LN):
                dve.wait_ge(s_lnsd, n)
                nc.vector.reciprocal(rstd[:, b, 0:t], std[:, b, 0:t]).then_inc(s_hot, 1)
                dve.wait_ge(s_hot, n)
                nc.vector.scalar_tensor_tensor(out=shift[:, b, 0:t], in0=mv[:, b, 0:t, 0], scalar=-1.0,
                                               in1=rstd[:, b, 0:t], op0=ALU.mult, op1=ALU.mult).then_inc(s_lnsh, 1)

            def ln_rest(b, n, t=LN):
                dve.wait_ge(s_lnh, n)
                nc.vector.tensor_tensor(ln_pair[:, b, 0:t, D:2 * D], ln_h[:, b, 0:t, :], ln_pair[:, b, 0:t, 0:D],
                                        ALU.subtract).then_inc(s_lnlo, 1)

            with dve.Fori(0, STEPS // 2) as j:
                for b in range(2):
                    ln_moments(b, 2 * j + b + 1, 16 * (j + 1))
                for b in range(2):
                    ln_shift(b, 2 * j + b + 1)
                for b in range(2):
                    ln_rest(b, 2 * j + b + 1)
            ln_moments(0, STEPS + 1, 16 * (STEPS // 2 + 1), 1)
            ln_shift(0, STEPS + 1, 1)
            ln_rest(0, STEPS + 1, 1)
            LNS = STEPS + 1

            dve.wait_ge(s_lnst[0], 16 * (STEPS // 2 + 1))
            dve.wait_ge(s_lnst[1], 16 * (STEPS // 2))
            nc.vector.memset(hot3[:, :, :, :], 0.0).then_inc(s_link, 1)
            chain[0] += 1
            dve.wait_ge(s_link, chain[0])
            flag = dve.value_load(flag_i[0:1, 0:1], min_val=0, max_val=1)
            dve.sem_inc(s_hot3, START)
            dve.sem_inc(s_add, START)
            dve.sem_inc(s_x1, START)
            dve.sem_inc(s_pair, START)
            LINKS = chain[0]

            def finish_first(n, b, loaded, step):
                if step == 1:
                    dve.wait_ge(s_proj, START + n + 1)
                    dve.wait_ge(s_ld[0][b], loaded)
                    nc.vector.tensor_tensor(xt[:, b, :], xt[:, b, :], ps[:, 6 + b, :], ALU.add).then_inc(s_x1, 1)
                    dve.wait_ge(s_x1, START + n + 1)
                    nc.vector.bn_stats(stats[:, b, 0, :], xt[:, b, :]).then_inc(s_link, 1)
                    dve.wait_ge(s_link, LINKS + 2 * n + 1)
                    dve.sem_inc(s_aggr_go, 1)
                    nc.vector.bn_aggr(mv[:, b, 0, :], stats[:, b, 0, :]).then_inc(s_mv, 1)
                if step == 2:
                    dve.wait_ge(s_std, n + 1)
                    nc.vector.reciprocal(rstd[:, b, 0:1], std[:, b, 0:1]).then_inc(s_link, 1)
                    dve.wait_ge(s_link, LINKS + 2 * n + 2)
                    nc.vector.scalar_tensor_tensor(out=shift[:, b, 0:1], in0=mv[:, b, 0, 0:1], scalar=-1.0,
                                                   in1=rstd[:, b, 0:1], op0=ALU.mult, op1=ALU.mult
                                                   ).then_inc(s_shift, 1)
                if step == 3:
                    dve.wait_ge(s_h, n + 1)
                    nc.vector.tensor_tensor(pair[:, b, D:2 * D], ht[:, b, :], pair[:, b, 0:D], ALU.subtract)
                    nc.vector.scalar_tensor_tensor(out=xt[:, b, :], in0=ht[:, b, :], scalar=1.0 / SCALE,
                                                   in1=xt[:, b, :], op0=ALU.mult, op1=ALU.add).then_inc(s_pair, 1)

            def finish_second(n, b, t, loaded, stored, step):
                if step == 1:
                    dve.wait_ge(s_proj, START + n + 1)
                    dve.wait_ge(s_wld, 48)
                    nc.vector.tensor_tensor(ht[:, b, :], ps[:, 6 + b, :], bias_t, ALU.add).then_inc(s_x1, 1)
                if step == 2:
                    dve.wait_ge(s_x1, START + n + 1)
                    dve.wait_ge(s_ld[1][b], loaded)
                    if stored is not None:
                        dve.wait_ge(s_ost[b], stored)
                    nc.vector.scalar_tensor_tensor(out=out_t[:, b, :], in0=ht[:, b, :], scalar=0.0,
                                                   in1=xt[:, b, :], op0=ALU.max, op1=ALU.add).then_inc(s_out, 1)

            def finish(l, n, b, t, loaded, stored, steps=(1, 2, 3)):
                for step in steps:
                    if l == 0:
                        finish_first(n, b, loaded, step)
                    else:
                        finish_second(n, b, t, loaded, stored, step)

            def clear(n, t):
                dve.wait_ge(s_stage, n + 1)
                nc.vector.tensor_copy(aggT[:, :, bass.ds(t * P, P)],
                                      zero[:, :].unsqueeze(2).to_broadcast([P, KD, P]))

            def make_hot(l, group, q):
                g, c = l * GROUPS + group, group * GC
                nc.vector.tensor_tensor(hot[:, q % 2], iota_w[:, :].unsqueeze(1).to_broadcast([P, GC, WIN]),
                                        relT[:, bass.ds(c, GC)].unsqueeze(2).to_broadcast([P, GC, WIN]),
                                        ALU.is_equal).then_inc(s_hot, 1)
                dve.wait_ge(s_hot, LNS + g + 1)
                dve.wait_ge(s_sum, START + g + 1 - GB)
                nc.vector.tensor_tensor(
                    hot3[:, q, :, 0:3 * WIN].rearrange("p c (a j) -> p c a j", a=3),
                    hot[:, q % 2].unsqueeze(2).to_broadcast([P, GC, 3, WIN]),
                    w3[:, bass.ds(c, GC), :].unsqueeze(3).to_broadcast([P, GC, 3, WIN]),
                    ALU.mult).then_inc(s_hot3, 1)

            with dve.If(flag == 1):
                dve.wait_ge(s_zero, 1)
                for k in range(AHEAD):
                    make_hot(0, k, k)
                for l in range(2):
                    def add_in(bl, q, base):
                        g = l * GROUPS + bl * GB + q
                        dve.wait_ge(s_fold, START + g + 1)
                        dve.wait_ge(s_add, START + g)
                        cols = aggT[:, :, bass.ds(base, WIN)]
                        nc.vector.tensor_tensor(cols, cols, ps[:, 4 + q % 2, 0:KD * WIN].rearrange(
                            "p (k j) -> p k j", k=KD), ALU.add).then_inc(s_add, 1)

                    def body(i, take, first):
                        base = []
                        for m in range(2):
                            bl = 2 * i + m
                            t = bl - LAG
                            n = l * TILES + t
                            base += nc.values_load_multi_w_load_instructions(
                                base_i[0:1, bass.ds(bl * GB, GB)], engines=(mybir.EngineType.DVE,),
                                min_val=0, max_val=N - 1,
                                skip_runtime_bounds_check_because="dst names nodes of the graph")[1]
                            for q in range(GB):
                                make_hot(l, bl * GB + q + AHEAD, (q + AHEAD) % GB)
                                k = m * GB + q - 2
                                if k >= 0:
                                    add_in(2 * i + k // GB, k % GB, base[k])
                                if take and q == 0 and l == 0:
                                    clear(n, t)
                                if take and q:
                                    finish(l, n, m, t, 16 * (i - LAG // 2 + 1),
                                           None if first else 16 * (i - LAG // 2), (q,))
                        for k in (2 * GB - 2, 2 * GB - 1):
                            add_in(2 * i + 1, k % GB, base[k])

                    with dve.Fori(0, LAG // 2) as i:
                        body(i, False, False)
                    body(LAG // 2, True, True)
                    with dve.Fori(LAG // 2 + 1, BLOCKS // 2) as i:
                        body(i, True, False)
                    for t in range(TILES - LATE, TILES):
                        n, b = l * TILES + t, t % 2
                        if l == 0:
                            clear(n, t)
                        finish(l, n, b, t, 16 * (t // 2 + 1), 16 * (t // 2))
            with dve.Else():
                for l in range(2):
                    dve.wait_ge(g_zero, 3 * l + 3)
                    with dve.Fori(0, CHUNKS) as c:
                        n = l * CHUNKS + c
                        LINKED = 6

                        def then(ins, k):
                            ins.then_inc(g_link, 1)
                            dve.wait_ge(g_link, LINKED * n + k)

                        node, weight = dstT[:, bass.ds(c, 1)], wT[:, bass.ds(c, 1)]
                        nc.vector.tensor_copy(dst_b, node.to_broadcast([P, P])).then_inc(g_dstb, 1)
                        dve.wait_ge(g_row, n + 1)
                        then(nc.vector.tensor_scalar(eq, ps[:, 1, 0:P], node, None, ALU.is_equal), 1)
                        then(nc.vector.tensor_tensor(dst_b, eq, below, ALU.mult), 2)
                        nc.vector.tensor_reduce(col[:, 0:1], dst_b, AX.X, ALU.add)
                        then(nc.vector.tensor_scalar(col[:, 1:2], node, float(N), None, ALU.is_lt), 3)
                        nc.vector.tensor_tensor(col[:, 2:3], node, trash, ALU.subtract)
                        then(nc.vector.tensor_scalar(col[:, 3:4], col[:, 0:1], 0.0, col[:, 1:2],
                                                     ALU.is_equal, ALU.mult), 4)
                        then(nc.vector.tensor_tensor(col[:, 4:5], col[:, 2:3], col[:, 3:4], ALU.mult), 5)
                        then(nc.vector.tensor_tensor(gen_to, col[:, 4:5], trash, ALU.add), 6)
                        dve.wait_ge(g_rows, 16 * n + 16)
                        nc.vector.tensor_tensor(ht[:, 0, :], rows[:, 0, 0:D], rows[:, 0, D:2 * D], ALU.add)
                        nc.vector.tensor_scalar(eqw, eq, weight, None, ALU.mult).then_inc(g_eq, 1)
                        dve.wait_ge(g_sum, n + 1)
                        dve.wait_ge(g_sc, 16 * n + 16)

                    for t in range(2):
                        finish(l, l * TILES + t, t, t, 16, None)
                    with dve.Fori(1, TILES // 2) as j:
                        for b in range(2):
                            finish(l, l * TILES + 2 * j + b, b, 2 * j + b, 16 * (j + 1), 16 * j)
                    finish(l, l * TILES + TILES - 1, 0, TILES - 1, 16 * (TILES // 2 + 1), 16 * (TILES // 2))



_INS = ["x", "src", "dst", "edge_weight", "L0_gnn_weight", "L1_gnn_W", "L1_gnn_b"]


def kernel(**inputs):
    import concourse.bacc as _bacc
    from concourse.bass_utils import run_bass_kernel_spmd as _run

    nc = _bacc.Bacc("TRN2", target_bir_lowering=False, num_devices=1)
    arrays, args = {}, []
    for name in _INS:
        a = np.ascontiguousarray(inputs[name])
        arrays[f"in_{name}_dram"] = a
        args.append(nc.dram_tensor(f"in_{name}_dram", a.shape, mybir.dt.from_np(a.dtype), kind="ExternalInput").ap())
    shape = tuple(inputs["x"].shape)
    args.append(nc.dram_tensor("out_0_dram", shape, mybir.dt.float32, kind="ExternalOutput").ap())
    gnn_kernel(nc, *args)
    r = _run(nc, [arrays], core_ids=[0])
    return r.results[0]["out_0_dram"]
```

```python
import numpy as np
import concourse.bass as bass
from concourse import mybir
from contextlib import ExitStack


def gnn_kernel(nc, x, src, dst, edge_weight, w_first, w_second, bias, out):
    f32, bf16, f16, i32 = mybir.dt.float32, mybir.dt.bfloat16, mybir.dt.float16, mybir.dt.int32
    ALU = mybir.AluOpType
    ACT = mybir.ActivationFunctionType
    AX = mybir.AxisListType

    P = 128
    N, D = x.shape
    E = src.shape[0]
    KD = D // P
    TILES = -(-N // P)
    REST = N - (TILES - 1) * P
    REAL = -(-E // P)
    GC, GB = 4, 4
    BLOCK = GC * GB
    BLOCKS = 2 * -(-REAL // (2 * BLOCK))
    CHUNKS = BLOCKS * BLOCK
    GROUPS = BLOCKS * GB
    PADS = CHUNKS * P - E
    NAT = -(-REAL // P)
    WIN = 42
    LAG = 6
    LATE = TILES - (BLOCKS - LAG)
    COLS = TILES * P + WIN
    NOWHERE = float(1 << 20)
    SCALE = 2048.0
    EPS = 1e-5
    START = 8
    AHEAD = 3
    LN = 2
    XB = 4
    STEPS = (TILES - 1) // LN
    ROUNDS = STEPS // XB
    assert ROUNDS * XB == STEPS and STEPS * LN == TILES - 1 and TILES % 2 and LATE == 3 and BLOCKS % 2 == 0 and LAG % 2 == 0

    ctx = ExitStack()
    with ctx:
        def sb(name, shape, dt):
            return ctx.enter_context(nc.sbuf_tensor(name, shape, dt))

        def sem(name):
            return ctx.enter_context(nc.semaphore(name))

        h_dram = [nc.dram_tensor(f"h{l}_dram", (N, 2 * D), f16, kind="Internal").ap() for l in range(2)]
        y_dram = nc.dram_tensor("y_dram", (N, D), f32, kind="Internal").ap()
        sum_dram = nc.dram_tensor("sum_dram", (N + P, D), f32, kind="Internal").ap()

        aggT = sb("aggT", [P, KD, COLS], f32)
        rows = sb("rows", [P, BLOCK, 2 * D], f16)
        idxT = sb("idxT", [P, CHUNKS + BLOCK], i32)
        dstT = sb("dstT", [P, CHUNKS], f32)
        wT = sb("wT", [P, CHUNKS], f32)
        relT = sb("relT", [P, CHUNKS + AHEAD * GC], bf16)
        w3 = sb("w3", [P, CHUNKS + AHEAD * GC, 3], bf16)
        idx_now = sb("idx_now", [P, 2, BLOCK], i32)
        wmat = sb("wmat", [P, 2, KD, D], f32)
        ident = sb("ident", [P, P], f32)
        fold = sb("fold", [P, WIN], f32)
        row0 = sb("row0", [P, P], f32)
        iota_w = sb("iota_w", [P, WIN], bf16)
        ones = sb("ones", [P, 1], f32)
        zero = sb("zero", [P, 1], f32)
        eps = sb("eps", [P, 1], f32)
        low = sb("low", [1, GROUPS], f32)
        base_i = sb("base_i", [1, GROUPS], i32)
        early = sb("early", [1, GROUPS], f32)
        counts = sb("counts", [P, 3], f32)
        flag_f = sb("flag_f", [1, 2], f32)
        flag_i = sb("flag_i", [1, 1], i32)
        stats = sb("stats", [P, XB, LN, 6], f32)
        mv = sb("mv", [P, XB, LN, 2], f32)
        std = sb("std", [P, XB, LN], f32)
        rstd = sb("rstd", [P, XB, LN], f32)
        shift = sb("shift", [P, XB, LN], f32)
        z = LN * D
        SCRATCH = (2 * XB + 2) * z
        scratch = sb("scratch", [P, SCRATCH], f32)

        ln_x = scratch[:, 0:XB * z].rearrange("p (b t d) -> p b t d", b=XB, t=LN)
        ln_pair = scratch[:, XB * z:2 * XB * z].bitcast(f16).rearrange("p (b t d) -> p b t d", b=XB, t=LN)
        ln_h = scratch[:, 2 * XB * z:SCRATCH].rearrange("p (b t d) -> p b t d", b=2, t=LN)
        at = [0]

        def part(words):
            at[0] += words
            assert at[0] <= SCRATCH
            return scratch[:, at[0] - words:at[0]]

        xt = part(3 * D).rearrange("p (b d) -> p b d", b=3)
        ht = part(3 * D).rearrange("p (b d) -> p b d", b=3)
        pair_words = part(3 * D)
        pair = pair_words.bitcast(f16).rearrange("p (b d) -> p b d", b=3)
        out_t = pair_words.rearrange("p (b d) -> p b d", b=3)
        stage = part(2 * D).rearrange("p (b k n) -> p b k n", b=2, k=KD)
        agg = part(2 * D).rearrange("p (b d) -> p b d", b=2)
        hot3 = part(4 * GC * P // 2).bitcast(bf16).rearrange("p (b c m) -> p b c m", b=4, c=GC)
        hot = part(2 * GC * WIN // 2).bitcast(bf16).rearrange("p (b c j) -> p b c j", b=2, c=GC)
        bias_t = part(D)
        dst_b, eq, eqw, below = (part(P) for _ in range(4))
        col = part(8)
        trash = part(1)
        gen_idx, gen_to = (part(1).bitcast(i32) for _ in range(2))

        temp = rows[:, :, :].rearrange("p a b -> p (a b)").bitcast(f32)
        w_nat = NAT * P

        def table(k):
            return temp[:, k * w_nat:(k + 1) * w_nat].rearrange("p (g e) -> p g e", g=NAT)

        src_nat, dst_nat = table(0).bitcast(i32), table(1).bitcast(i32)
        nat_f = [table(2), table(3), table(4)]
        rel_f = temp[:, 5 * w_nat:5 * w_nat + CHUNKS]
        rem = temp[:, 6 * w_nat:6 * w_nat + CHUNKS]
        junk = temp[:, 7 * w_nat:7 * w_nat + CHUNKS]

        ps = ctx.enter_context(nc.psum_tensor("ps", [P, 8, D], f32))
        turned = [ps[:, 2 * k:2 * k + 2, :].rearrange("p a b -> p (a b)") for k in range(3)]

        s_const = sem("constants_made")
        s_fill = sem("tables_filled")
        s_tab = sem("edge_tables_loaded")
        s_conv = sem("tables_as_float")
        s_turn = sem("tables_turned")
        s_dstT = sem("dst_table_ready")
        s_base = sem("bases_spread")
        s_cnt = sem("counts_ready")
        s_tot = sem("totals_ready")
        s_flag = sem("flag_ready")
        s_link = sem("vector_chain")
        s_wld = sem("weights_loaded")
        s_zero = sem("sums_zeroed")
        s_lnx = [sem(f"ln_x_loaded{b}") for b in range(XB)]
        s_lnst = [sem(f"ln_pair_stored{b}") for b in range(XB)]
        s_lnbn = sem("ln_halves")
        s_lnrs = sem("ln_rstd")
        s_wT = sem("weight_table_ready")
        s_w3 = sem("weight_parts")
        s_lnmv = sem("ln_moments")
        s_lnsd = sem("ln_std")
        s_lnsh = sem("ln_shift")
        s_lnh = sem("ln_h")
        s_lnlo = sem("ln_remainder")
        s_index_go = sem("pool_may_gather")
        s_aggr_go = sem("vector_may_aggregate")
        s_idx = sem("indices_staged")
        s_rows = [sem(f"rows_gathered{b}") for b in range(GB)]
        s_hot = sem("onehot_made")
        s_hot3 = sem("weights_in_place")
        s_sum = sem("group_summed")
        s_evac = sem("sum_copied")
        s_fold = sem("group_folded")
        s_add = sem("group_added")
        s_stage = sem("tile_staged")
        s_clear = sem("tile_cleared")
        s_proj = sem("tile_projected")
        s_x1 = sem("residual_added")
        s_bn = sem("tile_halves")
        s_mv = sem("tile_moments")
        s_rstd = sem("tile_rstd")
        s_std = sem("tile_std")
        s_shift = sem("tile_shift")
        s_h = sem("tile_h")
        s_pair = sem("tile_pair")
        s_out = sem("tile_out")
        s_ld = [[sem(f"tile_loaded{l}{b}") for b in range(3)] for l in range(2)]
        s_hst = [sem(f"h_stored{b}") for b in range(3)]
        s_yst = [sem(f"y_stored{b}") for b in range(3)]
        s_ost = [sem(f"out_stored{b}") for b in range(3)]
        g_link = sem("g_vector_chain")
        g_zero = sem("g_zero_tile")
        g_ones = sem("g_ones_made")
        g_zst = sem("g_sums_cleared")
        g_idx = sem("g_index_copied")
        g_rows = sem("g_rows_gathered")
        g_dstb = sem("g_dst_spread")
        g_row = sem("g_dst_row")
        g_eq = sem("g_matrix_ready")
        g_sum = sem("g_chunk_summed")
        g_msg = sem("g_chunk_copied")
        g_sc = sem("g_chunk_added")
        g_ld = sem("g_tile_loaded")
        g_tr = sem("g_tile_turned")

        block = ctx.enter_context(nc.Block())
        wm = [w_first, w_second]
        PAIRS = TILES // 2

        def stored_all(b):
            return 16 * (1 if b == 2 else PAIRS)

        def ln_stored_all(b):
            return 16 * (ROUNDS + (b == 0))

        def whole(t):
            return t * P, (REST if isinstance(t, int) and t == TILES - 1 else P)

        def node_rows(ap, t):
            n0, n = whole(t)
            return ap[bass.ds(n0, n), :]

        @block.sync
        def _(sp):
            xg = x[0:STEPS * LN * P, :].rearrange("(s t p) d -> s p t d", t=LN, p=P)
            hg = h_dram[0][0:STEPS * LN * P, :].rearrange("(s t p) d -> s p t d", t=LN, p=P)

            def step_of(ap, step):
                return ap[step] if isinstance(step, int) else ap[bass.ds(step, 1)].rearrange("s p t d -> (s p) t d")

            def ln_load(step, b):
                sp.dma_start(ln_x[:, b], step_of(xg, step)).then_inc(s_lnx[b], 16)

            def ln_store(step, b):
                sp.wait_ge(s_lnlo, step + 1)
                sp.dma_start(step_of(hg, step), ln_pair[:, b]).then_inc(s_lnst[b], 16)

            for b in range(XB):
                ln_load(b, b)
            sp.wait_ge(s_fill, 1)
            full = (NAT - 1) * P * P
            more = (E - full) // P
            for nat, edges in ((dst_nat, dst), (src_nat, src), (nat_f[2], edge_weight)):
                sp.dma_start(nat[:, 0:NAT - 1, :], edges[0:full].rearrange("(g p e) -> p g e", p=P, e=P)
                             ).then_inc(s_tab, 16)
                sp.dma_start(nat[0:more, NAT - 1, :], edges[full:full + more * P].rearrange("(p e) -> p e", e=P)
                             ).then_inc(s_tab, 16)
                sp.dma_start(nat[more:more + 1, NAT - 1, 0:E - full - more * P],
                             edges[full + more * P:E].rearrange("(p e) -> p e", p=1)).then_inc(s_tab, 16)
            with sp.Fori(0, ROUNDS - 1) as j:
                for b in range(XB):
                    sp.wait_ge(s_lnh, XB * j + b + 1)
                    ln_load(XB * (j + 1) + b, b)
                    ln_store(XB * j + b, b)
            sp.wait_ge(s_lnh, STEPS - XB + 1)
            sp.dma_start(ln_x[0:REST, 0, 0, :], x[N - REST:N, :]).then_inc(s_lnx[0], 16)
            for b in range(XB):
                ln_store(STEPS - XB + b, b)
            sp.wait_ge(s_lnlo, STEPS + 1)
            sp.dma_start(h_dram[0][N - REST:N, :], ln_pair[0:REST, 0, 0, :]).then_inc(s_lnst[0], 16)
            for l in range(2):
                sp.dma_start(wmat[:, l], wm[l].rearrange("(k p) d -> p k d", p=P)).then_inc(s_wld, 16)
            for b in range(XB):
                sp.wait_ge(s_lnst[b], ln_stored_all(b))

            def load(l, t, b):
                n0, n = whole(t)
                sp.dma_start(xt[0:n, b, :], node_rows(x if l == 0 else y_dram, t)).then_inc(s_ld[l][b], 16)

            def store_first(t, b, k):
                n0, n = whole(t)
                sp.wait_ge(s_pair, START + t + 1)
                sp.dma_start(node_rows(h_dram[1], t), pair[0:n, b, :]).then_inc(s_hst[b], 16)
                sp.dma_start(node_rows(y_dram, t), xt[0:n, b, :]).then_inc(s_yst[b], 16)
                if k is not None:
                    sp.wait_ge(s_yst[b], 16 * k)

            def store_second(t, b):
                n0, n = whole(t)
                sp.wait_ge(s_out, t + 1)
                sp.dma_start(node_rows(out, t), out_t[0:n, b, :]).then_inc(s_ost[b], 16)

            for l in range(2):
                load(l, 0, 0)
                load(l, 1, 1)
                load(l, TILES - 1, 2)
                if l == 0:
                    sp.dma_start(bias_t, bias.rearrange("(a d) -> a d", a=1).to_broadcast([P, D])).then_inc(s_wld, 16)
                with sp.Fori(0, PAIRS - 1) as j:
                    for b in range(2):
                        if l == 0:
                            store_first(2 * j + b, b, j + 1)
                        else:
                            store_second(2 * j + b, b)
                        load(l, 2 * j + b + 2, b)
                for t, b in ((TILES - 3, 0), (TILES - 2, 1), (TILES - 1, 2)):
                    if l == 0:
                        store_first(t, b, None)
                    else:
                        store_second(t, b)
                for b in range(3):
                    if l == 0:
                        sp.wait_ge(s_hst[b], stored_all(b))
                        sp.wait_ge(s_yst[b], stored_all(b))
                    else:
                        sp.wait_ge(s_ost[b], stored_all(b))

        @block.gpsimd
        def _(pool):
            nc.gpsimd.memset(ident[:, :], 0.0).then_inc(s_const, 1)
            nc.gpsimd.memset(fold[:, :], 0.0).then_inc(s_const, 1)
            nc.gpsimd.memset(row0[:, :], 0.0).then_inc(s_const, 1)
            pool.wait_ge(s_const, 3)
            nc.gpsimd.affine_select(out=ident[:, :], in_=ident[:, :], compare_op=ALU.not_equal, fill=1.0,
                                    base=0, pattern=[[-1, P]], channel_multiplier=1).then_inc(s_const, 1)
            for k in range(3):
                nc.gpsimd.affine_select(out=fold[:, :], in_=fold[:, :], compare_op=ALU.not_equal,
                                        fill=1.0 / SCALE, base=-k * WIN, pattern=[[-1, WIN]],
                                        channel_multiplier=1).then_inc(s_const, 1)
                pool.wait_ge(s_const, 5 + k)
            nc.gpsimd.affine_select(out=row0[:, :], in_=row0[:, :], compare_op=ALU.not_equal, fill=1.0,
                                    base=0, pattern=[[0, P]], channel_multiplier=1).then_inc(s_const, 1)
            nc.gpsimd.iota(iota_w[:, :], pattern=[[1, WIN]], base=0, channel_multiplier=0,
                           allow_small_or_imprecise_dtypes=True).then_inc(s_const, 1)
            nc.gpsimd.iota(low[:, :], pattern=[[P, BLOCKS], [0, GB]], base=-(LAG - 2) * P, channel_multiplier=0,
                           allow_small_or_imprecise_dtypes=True).then_inc(s_const, 1)
            pool.wait_ge(s_wT, 1)
            nc.gpsimd.tensor_copy(w3[:, 0:CHUNKS, 0], wT[:, :]).then_inc(s_w3, 1)
            pool.wait_ge(s_w3, 1)
            nc.gpsimd.tensor_tensor(rem, wT[:, :], w3[:, 0:CHUNKS, 0], ALU.subtract).then_inc(s_w3, 1)
            pool.wait_ge(s_w3, 2)
            nc.gpsimd.tensor_copy(w3[:, 0:CHUNKS, 1], rem).then_inc(s_w3, 1)
            pool.wait_ge(s_w3, 3)
            nc.gpsimd.tensor_tensor(rem, rem, w3[:, 0:CHUNKS, 1], ALU.subtract).then_inc(s_w3, 1)
            pool.wait_ge(s_w3, 4)
            nc.gpsimd.tensor_copy(w3[:, 0:CHUNKS, 2], rem).then_inc(s_w3, 1)
            pool.wait_ge(s_w3, 5)
            nc.gpsimd.tensor_copy(w3[:, CHUNKS:CHUNKS + AHEAD * GC, :], w3[:, 0:AHEAD * GC, :]).then_inc(s_w3, 1)
            nc.gpsimd.memset(aggT[:, :, :], 0.0).then_inc(s_zero, 1)

            pool.wait_ge(s_flag, 1)
            flag = pool.value_load(flag_i[0:1, 0:1], min_val=0, max_val=1)

            def h_ready(l):
                if l == 0:
                    for b in range(XB):
                        pool.wait_ge(s_lnst[b], ln_stored_all(b))
                else:
                    for b in range(3):
                        pool.wait_ge(s_hst[b], stored_all(b))

            def before_indexed():
                pool.sem_inc(s_index_go, 1)

            with pool.If(flag == 1):
                for l in range(2):
                    h_ready(l)
                    with pool.Fori(0, BLOCKS // 2) as i:
                        for m in range(2):
                            bl = 2 * i + m
                            pool.wait_ge(s_idx, l * BLOCKS + bl + 1)
                            for q in range(GB):
                                g = l * GROUPS + bl * GB + q
                                pool.wait_ge(s_sum, START + g + 1 - GB)
                                before_indexed()
                                for c in range(GC):
                                    k = q * GC + c
                                    pool.indirect_dma_start(
                                        out=rows[:, k, :], out_offset=None, in_=h_dram[l][:, :],
                                        in_offset=bass.IndirectOffsetOnAxis(ap=idx_now[:, m, k:k + 1], axis=0),
                                    ).then_inc(s_rows[q], 16)
            with pool.Else():
                for l in range(2):
                    h_ready(l)
                    if l == 1:
                        pool.wait_ge(g_ld, 16 * TILES)
                    nc.gpsimd.memset(agg[:, 0, :], 0.0).then_inc(g_zero, 1)
                    nc.gpsimd.memset(below, 1.0).then_inc(g_ones, 1)
                    pool.wait_ge(g_ones, l + 1)
                    nc.gpsimd.affine_select(out=below, in_=below, compare_op=ALU.is_gt, fill=0.0, base=0,
                                            pattern=[[-1, P]], channel_multiplier=1).then_inc(g_zero, 1)
                    nc.gpsimd.iota(trash, pattern=[[0, 1]], base=N, channel_multiplier=1,
                                   allow_small_or_imprecise_dtypes=True).then_inc(g_zero, 1)
                    pool.wait_ge(g_zero, 3 * l + 3)
                    with pool.Fori(0, TILES) as t:
                        pool.dma_start(sum_dram[bass.ds(t * P, P), :], agg[:, 0, :]).then_inc(g_zst, 16)
                    pool.dma_start(sum_dram[TILES * P:N + P, :], agg[0:N + P - TILES * P, 0, :]).then_inc(g_zst, 16)
                    pool.wait_ge(g_zst, 16 * (TILES + 1) * (l + 1))
                    with pool.Fori(0, CHUNKS) as c:
                        n = l * CHUNKS + c
                        nc.gpsimd.tensor_copy(gen_idx, idxT[:, bass.ds(c, 1)]).then_inc(g_idx, 1)
                        pool.wait_ge(g_idx, n + 1)
                        before_indexed()
                        pool.indirect_dma_start(
                            out=rows[:, 0, :], out_offset=None, in_=h_dram[l][:, :],
                            in_offset=bass.IndirectOffsetOnAxis(ap=gen_idx, axis=0)).then_inc(g_rows, 16)
                        pool.wait_ge(g_msg, n + 1)
                        before_indexed()
                        pool.indirect_dma_start(
                            out=sum_dram[:, :], out_offset=bass.IndirectOffsetOnAxis(ap=gen_to, axis=0),
                            in_=agg[:, 1, :], in_offset=None, compute_op=ALU.add).then_inc(g_sc, 16)
                        pool.wait_ge(g_sc, 16 * n + 16)

        @block.scalar
        def _(act):
            def ln_std(b, n, t=LN):
                act.wait_ge(s_lnmv, n)
                act.activation(std[:, b, 0:t], mv[:, b, 0:t, 1], ACT.Sqrt, bias=eps[:, :],
                               scale=1.0 / SCALE ** 2).then_inc(s_lnsd, 1)

            def ln_relu(b, k, used, stored, t=LN):
                act.wait_ge(s_lnsh, k + 1)
                if used:
                    act.wait_ge(s_lnlo, k - 1)
                if stored is not None:
                    act.wait_ge(s_lnst[b], stored)
                for i in range(t):
                    for o in (ln_h[:, b % 2, i, :], ln_pair[:, b, i, 0:D]):
                        last = act.activation(o, ln_x[:, b, i, :], ACT.Relu,
                                              bias=shift[:, b, i:i + 1], scale=rstd[:, b, i:i + 1])
                last.then_inc(s_lnh, 1)

            def ln_round(j, first, last):
                for b in range(XB):
                    k = XB * j + b
                    ln_std((b + 1) % XB, k + 2, 1 if last and b == XB - 1 else LN)
                    ln_relu(b, k, not first or b >= 2, None if first else 16 * j)

            ln_std(0, 1)
            ln_round(0, True, False)
            act.wait_ge(s_turn, 3)
            act.activation(wT[:, :], turned[2][:, 0:CHUNKS], ACT.Copy).then_inc(s_wT, 1)
            with act.Fori(1, ROUNDS - 1) as j:
                ln_round(j, False, False)
            ln_round(ROUNDS - 1, False, True)
            ln_relu(0, STEPS, True, 16 * ROUNDS, 1)

            act.wait_ge(s_flag, 1)
            flag = act.value_load(flag_i[0:1, 0:1], min_val=0, max_val=1)

            def stage_tile(n, b, t, added):
                act.wait_ge(s_add, added)
                act.wait_ge(s_proj, START + n - 1)
                act.activation(stage[:, b], aggT[:, :, bass.ds(t * P, P)], ACT.Copy).then_inc(s_stage, 1)

            def std_tile(n, b):
                act.wait_ge(s_mv, n + 1)
                act.activation(std[:, b, 0:1], mv[:, b, 0, 1:2], ACT.Sqrt, bias=eps[:, :],
                               scale=1.0 / SCALE ** 2).then_inc(s_std, 1)

            def relu_tile(n, b, stored):
                act.wait_ge(s_shift, n + 1)
                act.wait_ge(s_pair, START + n - 1)
                if stored is not None:
                    act.wait_ge(s_hst[b], stored)
                act.activation(ht[:, b, :], xt[:, b, :], ACT.Relu, bias=shift[:, b, 0:1], scale=rstd[:, b, 0:1])
                act.activation(pair[:, b, 0:D], xt[:, b, :], ACT.Relu, bias=shift[:, b, 0:1],
                               scale=rstd[:, b, 0:1]).then_inc(s_h, 1)

            act.sem_inc(s_evac, START)
            with act.If(flag == 1):
                for l in range(2):
                    def body(i, take, first):
                        for m in range(2):
                            bl = 2 * i + m
                            t = bl - LAG
                            n = l * TILES + t
                            if take:
                                stage_tile(n, m, t, START + l * GROUPS + GB * (bl - 1))
                            for q in range(GB):
                                g = l * GROUPS + bl * GB + q
                                act.wait_ge(s_sum, START + g + 1)
                                act.wait_ge(s_fold, START + g - 1)
                                act.activation(agg[:, q % 2, :], ps[:, q, :], ACT.Copy).then_inc(s_evac, 1)
                                if take and l == 0 and q == 1:
                                    std_tile(n, m)
                                if take and l == 0 and q == 2:
                                    relu_tile(n, m, None if first else 16 * (i - LAG // 2))

                    with act.Fori(0, LAG // 2) as i:
                        body(i, False, False)
                    body(LAG // 2, True, True)
                    with act.Fori(LAG // 2 + 1, BLOCKS // 2) as i:
                        body(i, True, False)
                    n, t = l * TILES + TILES - 3, TILES - 3
                    stage_tile(n, 0, t, START + l * GROUPS + GB * (BLOCKS - 1))
                    stage_tile(n + 1, 1, t + 1, START + (l + 1) * GROUPS)
                    if l == 0:
                        std_tile(n, 0)
                        relu_tile(n, 0, 16 * (PAIRS - 1))
                    stage_tile(n + 2, 0, t + 2, START + (l + 1) * GROUPS)
                    if l == 0:
                        std_tile(n + 1, 1)
                        relu_tile(n + 1, 1, 16 * (PAIRS - 1))
                        std_tile(n + 2, 2)
                        relu_tile(n + 2, 2, None)
            with act.Else():
                for l in range(2):
                    with act.Fori(0, CHUNKS) as c:
                        n = l * CHUNKS + c
                        act.wait_ge(g_sum, n + 1)
                        act.activation(agg[:, 1, :], ps[:, 0, :], ACT.Copy, scale=1.0 / SCALE).then_inc(g_msg, 1)

                    def gen_tile(t, b, stored, buf=None):
                        n = l * TILES + t
                        buf = b if buf is None else buf
                        act.dma_start(agg[:, 0, :], sum_dram[bass.ds(t * P, P), :]).then_inc(g_ld, 16)
                        act.wait_ge(g_tr, n + 1)
                        act.wait_ge(s_proj, START + n - 1)
                        act.activation(stage[:, b], ps[:, 4, :].rearrange("p (k n) -> p k n", k=KD), ACT.Copy
                                       ).then_inc(s_stage, 1)
                        if l == 0:
                            std_tile(n, buf)
                            relu_tile(n, buf, stored)

                    act.wait_ge(g_sc, 16 * CHUNKS * (l + 1))
                    for b in range(2):
                        gen_tile(b, b, None)
                    with act.Fori(1, TILES // 2) as j:
                        for b in range(2):
                            gen_tile(2 * j + b, b, 16 * j)
                    gen_tile(TILES - 1, 0, None, 2)

        @block.tensor
        def _(pe):
            pe.wait_ge(s_const, 4)
            for k, name in ((1, "dst"), (0, "src"), (2, "weight")):
                if name == "weight":
                    pe.wait_ge(s_tab, 9 * 16)
                else:
                    pe.wait_ge(s_conv, 1 + (k == 0))
                for g in range(NAT):
                    last = nc.tensor.transpose(turned[k][:, g * P:(g + 1) * P], nat_f[k][:, g, :], ident[:, :])
                last.then_inc(s_turn, 1)
            pe.wait_ge(s_const, 8)
            pe.wait_ge(s_dstT, 1)
            nc.tensor.matmul(ps[:, 6, 0:GROUPS], row0[:, :], dstT[:, ::GC], start=True, stop=True).then_inc(s_base, 1)
            pe.wait_ge(s_cnt, 1)
            nc.tensor.matmul(ps[0:1, 7, 0:3], ones[:, :], counts[:, :], start=True, stop=True).then_inc(s_tot, 1)
            pe.wait_ge(s_wld, 48)

            pe.wait_ge(s_flag, 1)
            flag = pe.value_load(flag_i[0:1, 0:1], min_val=0, max_val=1)
            pe.sem_inc(s_sum, START)
            pe.sem_inc(s_fold, START)
            pe.sem_inc(s_proj, START)

            def project(l, n, b):
                pe.wait_ge(s_stage, n + 1)
                pe.wait_ge(s_x1, START + n - 1)
                for k in range(KD):
                    last = nc.tensor.matmul(ps[:, 6 + b, :], stage[:, b, k, :], wmat[:, l, k, :],
                                            start=(k == 0), stop=(k == KD - 1))
                last.then_inc(s_proj, 1)

            with pe.If(flag == 1):
                for l in range(2):
                    def add_up(bl, q):
                        g = l * GROUPS + bl * GB + q
                        pe.wait_ge(s_rows[q], 16 * GC * (l * BLOCKS + bl + 1))
                        pe.wait_ge(s_hot3, START + g + 1)
                        pe.wait_ge(s_evac, START + g + 1 - GB)
                        for c in range(GC):
                            for part_ in range(2):
                                last = nc.tensor.matmul(
                                    ps[:, q, :], hot3[:, q, c, :],
                                    rows[:, q * GC + c, part_ * D:(part_ + 1) * D],
                                    start=(c == 0 and part_ == 0), stop=(c == GC - 1 and part_ == 1))
                        last.then_inc(s_sum, 1)

                    def fold_up(bl, q):
                        g = l * GROUPS + bl * GB + q
                        pe.wait_ge(s_evac, START + g + 1)
                        pe.wait_ge(s_add, START + g - 1)
                        for k in range(KD):
                            last = nc.tensor.matmul(ps[:, 4 + q % 2, k * WIN:(k + 1) * WIN],
                                                    agg[:, q % 2, k * P:(k + 1) * P], fold[:, :],
                                                    start=True, stop=True)
                        last.then_inc(s_fold, 1)

                    def body(i, take):
                        for m in range(2):
                            bl = 2 * i + m
                            for q in range(GB):
                                add_up(bl, q)
                                if take and q == 1:
                                    project(l, l * TILES + bl - LAG, m)
                                if q or m:
                                    fold_up(bl if q else bl - 1, (q - 1) % GB)
                        fold_up(2 * i + 1, GB - 1)

                    with pe.Fori(0, LAG // 2) as i:
                        body(i, False)
                    with pe.Fori(LAG // 2, BLOCKS // 2) as i:
                        body(i, True)
                    for t in range(TILES - LATE, TILES):
                        project(l, l * TILES + t, t % 2)
            with pe.Else():
                for l in range(2):
                    with pe.Fori(0, CHUNKS) as c:
                        n = l * CHUNKS + c
                        pe.wait_ge(g_dstb, n + 1)
                        nc.tensor.matmul(ps[:, 1, 0:P], dst_b, ident[:, :], start=True, stop=True).then_inc(g_row, 1)
                        pe.wait_ge(g_eq, n + 1)
                        nc.tensor.matmul(ps[:, 0, :], eqw, ht[:, 0, :], start=True, stop=True).then_inc(g_sum, 1)

                    def gen_tile(t, b):
                        n = l * TILES + t
                        pe.wait_ge(g_ld, 16 * (n + 1))
                        for k in range(KD):
                            last = nc.tensor.transpose(ps[:, 4, k * P:(k + 1) * P], agg[:, 0, k * P:(k + 1) * P],
                                                       ident[:, :])
                        last.then_inc(g_tr, 1)
                        project(l, n, b)

                    with pe.Fori(0, TILES // 2) as j:
                        for b in range(2):
                            gen_tile(2 * j + b, b)
                    gen_tile(TILES - 1, 0)

        @block.vector
        def _(dve):
            nc.vector.memset(src_nat[:, NAT - 1, :], 0)
            nc.vector.memset(dst_nat[:, NAT - 1, :], int(NOWHERE))
            nc.vector.memset(nat_f[2][:, NAT - 1, :], 0.0).then_inc(s_fill, 1)
            nc.vector.memset(idxT[:, :], 0)
            nc.vector.memset(counts[:, :], 0.0)
            nc.vector.memset(ones[:, :], 1.0)
            nc.vector.memset(zero[:, :], 0.0)
            nc.vector.memset(eps[:, :], EPS / SCALE ** 2)
            chain = [0]

            def link(ins):
                chain[0] += 1
                ins.then_inc(s_link, 1)
                dve.wait_ge(s_link, chain[0])

            nc.vector.memset(junk, 0.0)

            def ln_moments(b, k, loaded, t=LN):
                dve.wait_ge(s_lnx[b], loaded)
                for i in range(t):
                    last = nc.vector.bn_stats(stats[:, b, i, :], ln_x[:, b, i, :])
                last.then_inc(s_lnbn, 1)
                dve.wait_ge(s_lnbn, k + 1)
                dve.sem_inc(s_aggr_go, 1)
                for i in range(t):
                    last = nc.vector.bn_aggr(mv[:, b, i, :], stats[:, b, i, :])
                last.then_inc(s_lnmv, 1)

            def ln_shift(b, k, t=LN):
                dve.wait_ge(s_lnsd, k + 1)
                nc.vector.reciprocal(rstd[:, b, 0:t], std[:, b, 0:t]).then_inc(s_lnrs, 1)
                dve.wait_ge(s_lnrs, k + 1)
                nc.vector.scalar_tensor_tensor(out=shift[:, b, 0:t], in0=mv[:, b, 0:t, 0], scalar=-1.0,
                                               in1=rstd[:, b, 0:t], op0=ALU.mult, op1=ALU.mult).then_inc(s_lnsh, 1)

            def ln_rest(b, k, t=LN):
                dve.wait_ge(s_lnh, k + 1)
                nc.vector.tensor_tensor(ln_pair[:, b, 0:t, D:2 * D], ln_h[:, b % 2, 0:t, :],
                                        ln_pair[:, b, 0:t, 0:D], ALU.subtract).then_inc(s_lnlo, 1)

            def ln_round(j, last):
                for b in range(XB):
                    k = XB * j + b
                    if not last or b < XB - 1:
                        ln_moments((b + 2) % XB, k + 2, 16 * (j + 1 + (b + 2) // XB),
                                   1 if last and b == XB - 2 else LN)
                    ln_shift((b + 1) % XB, k + 1, 1 if last and b == XB - 1 else LN)
                    ln_rest(b, k)

            ln_moments(0, 0, 16)
            ln_moments(1, 1, 16)
            ln_shift(0, 0)
            ln_round(0, False)

            dve.wait_ge(s_tab, 9 * 16)
            nc.vector.tensor_copy(nat_f[1], dst_nat).then_inc(s_conv, 1)
            nc.vector.tensor_copy(nat_f[0], src_nat).then_inc(s_conv, 1)
            dve.wait_ge(s_turn, 1)
            nc.vector.tensor_copy(dstT[:, :], turned[1][:, 0:CHUNKS]).then_inc(s_dstT, 1)
            dve.wait_ge(s_turn, 3)
            link(nc.vector.tensor_copy(idxT[:, 0:CHUNKS], turned[0][:, 0:CHUNKS]))
            nc.vector.tensor_copy(idxT[:, CHUNKS:CHUNKS + BLOCK], idxT[:, 0:BLOCK])
            dve.wait_ge(s_base, 1)
            link(nc.vector.tensor_tensor(rel_f.rearrange("p (g c) -> p g c", c=GC),
                                         dstT[:, :].rearrange("p (g c) -> p g c", c=GC),
                                         ps[:, 6, 0:GROUPS].unsqueeze(2).to_broadcast([P, GROUPS, GC]),
                                         ALU.subtract))
            link(nc.vector.tensor_copy(relT[:, 0:CHUNKS], rel_f))
            nc.vector.tensor_copy(relT[:, CHUNKS:CHUNKS + AHEAD * GC], relT[:, 0:AHEAD * GC])
            nc.vector.tensor_copy(base_i[:, :], ps[0:1, 6, 0:GROUPS])
            link(nc.vector.tensor_scalar(junk, rel_f, float(WIN), 0.0, ALU.is_ge, ALU.add, accum_out=counts[:, 0:1]))
            link(nc.vector.tensor_scalar(junk, rel_f, 0.0, 0.0, ALU.is_lt, ALU.add, accum_out=counts[:, 1:2]))
            dve.wait_ge(s_const, 10)
            link(nc.vector.tensor_tensor(early[:, :], ps[0:1, 6, 0:GROUPS], low[:, :], ALU.is_lt))
            nc.vector.tensor_reduce(counts[0:1, 2:3], early[:, :], AX.X, ALU.add).then_inc(s_cnt, 1)
            dve.wait_ge(s_tot, 1)
            link(nc.vector.tensor_scalar(flag_f[:, 1:2], ps[0:1, 7, 2:3], float(P * CHUNKS), None, ALU.mult))
            link(nc.vector.tensor_scalar(flag_f[:, 0:1], ps[0:1, 7, 0:1], flag_f[:, 1:2], None, ALU.add))
            link(nc.vector.tensor_scalar(flag_f[:, 1:2], flag_f[:, 0:1], ps[0:1, 7, 1:2], float(PADS), ALU.add, ALU.is_equal))
            nc.vector.tensor_copy(flag_i[:, :], flag_f[:, 1:2]).then_inc(s_flag, 1)

            with dve.Fori(1, ROUNDS - 1) as j:
                ln_round(j, False)
            ln_round(ROUNDS - 1, True)
            ln_rest(0, STEPS, 1)

            for b in range(XB):
                dve.wait_ge(s_lnst[b], ln_stored_all(b))
            nc.vector.memset(hot3[:, :, :, :], 0.0).then_inc(s_link, 1)
            chain[0] += 1
            dve.wait_ge(s_link, chain[0])
            flag = dve.value_load(flag_i[0:1, 0:1], min_val=0, max_val=1)
            dve.sem_inc(s_hot3, START)
            dve.sem_inc(s_add, START)
            dve.sem_inc(s_x1, START)
            dve.sem_inc(s_pair, START)

            def finish_first(n, b, buf, loaded, step):
                if step == 1:
                    dve.wait_ge(s_proj, START + n + 1)
                    dve.wait_ge(s_ld[0][buf], loaded)
                    nc.vector.tensor_tensor(xt[:, buf, :], xt[:, buf, :], ps[:, 6 + b, :], ALU.add).then_inc(s_x1, 1)
                    dve.wait_ge(s_x1, START + n + 1)
                    nc.vector.bn_stats(stats[:, buf, 0, :], xt[:, buf, :]).then_inc(s_bn, 1)
                    dve.wait_ge(s_bn, n + 1)
                    dve.sem_inc(s_aggr_go, 1)
                    nc.vector.bn_aggr(mv[:, buf, 0, :], stats[:, buf, 0, :]).then_inc(s_mv, 1)
                if step == 2:
                    dve.wait_ge(s_std, n + 1)
                    nc.vector.reciprocal(rstd[:, buf, 0:1], std[:, buf, 0:1]).then_inc(s_rstd, 1)
                    dve.wait_ge(s_rstd, n + 1)
                    nc.vector.scalar_tensor_tensor(out=shift[:, buf, 0:1], in0=mv[:, buf, 0, 0:1], scalar=-1.0,
                                                   in1=rstd[:, buf, 0:1], op0=ALU.mult, op1=ALU.mult
                                                   ).then_inc(s_shift, 1)
                if step == 3:
                    dve.wait_ge(s_h, n + 1)
                    nc.vector.tensor_tensor(pair[:, buf, D:2 * D], ht[:, buf, :], pair[:, buf, 0:D], ALU.subtract)
                    nc.vector.scalar_tensor_tensor(out=xt[:, buf, :], in0=ht[:, buf, :], scalar=1.0 / SCALE,
                                                   in1=xt[:, buf, :], op0=ALU.mult, op1=ALU.add).then_inc(s_pair, 1)

            def finish_second(n, b, buf, loaded, stored, step):
                if step == 1:
                    dve.wait_ge(s_proj, START + n + 1)
                    dve.wait_ge(s_wld, 48)
                    nc.vector.tensor_tensor(ht[:, buf, :], ps[:, 6 + b, :], bias_t, ALU.add).then_inc(s_x1, 1)
                if step == 2:
                    dve.wait_ge(s_x1, START + n + 1)
                    dve.wait_ge(s_ld[1][buf], loaded)
                    if stored is not None:
                        dve.wait_ge(s_ost[buf], stored)
                    nc.vector.scalar_tensor_tensor(out=out_t[:, buf, :], in0=ht[:, buf, :], scalar=0.0,
                                                   in1=xt[:, buf, :], op0=ALU.max, op1=ALU.add).then_inc(s_out, 1)

            def finish(l, n, b, buf, loaded, stored, steps=(1, 2, 3)):
                for step in steps:
                    if l == 0:
                        finish_first(n, b, buf, loaded, step)
                    else:
                        finish_second(n, b, buf, loaded, stored, step)

            def clear(n, t):
                dve.wait_ge(s_stage, n + 1)
                nc.vector.tensor_copy(aggT[:, :, bass.ds(t * P, P)],
                                      zero[:, :].unsqueeze(2).to_broadcast([P, KD, P]))

            def make_hot(l, group, q):
                g, c = l * GROUPS + group, group * GC
                nc.vector.tensor_tensor(hot[:, q % 2], iota_w[:, :].unsqueeze(1).to_broadcast([P, GC, WIN]),
                                        relT[:, bass.ds(c, GC)].unsqueeze(2).to_broadcast([P, GC, WIN]),
                                        ALU.is_equal).then_inc(s_hot, 1)
                dve.wait_ge(s_hot, g + 1)
                dve.wait_ge(s_sum, START + g + 1 - GB)
                nc.vector.tensor_tensor(
                    hot3[:, q, :, 0:3 * WIN].rearrange("p c (a j) -> p c a j", a=3),
                    hot[:, q % 2].unsqueeze(2).to_broadcast([P, GC, 3, WIN]),
                    w3[:, bass.ds(c, GC), :].unsqueeze(3).to_broadcast([P, GC, 3, WIN]),
                    ALU.mult).then_inc(s_hot3, 1)

            def stage_indices(l, bl, b):
                nc.vector.tensor_copy(idx_now[:, b, :], idxT[:, bass.ds(bl * BLOCK, BLOCK)]).then_inc(s_idx, 1)

            with dve.If(flag == 1):
                stage_indices(0, 0, 0)
                dve.wait_ge(s_zero, 1)
                dve.wait_ge(s_w3, 6)
                for k in range(AHEAD):
                    make_hot(0, k, k)
                for l in range(2):
                    def add_in(bl, q, base):
                        g = l * GROUPS + bl * GB + q
                        dve.wait_ge(s_fold, START + g + 1)
                        dve.wait_ge(s_add, START + g)
                        cols = aggT[:, :, bass.ds(base, WIN)]
                        nc.vector.tensor_tensor(cols, cols, ps[:, 4 + q % 2, 0:KD * WIN].rearrange(
                            "p (k j) -> p k j", k=KD), ALU.add).then_inc(s_add, 1)

                    def body(i, take, first):
                        base = []
                        for m in range(2):
                            bl = 2 * i + m
                            t = bl - LAG
                            n = l * TILES + t
                            base += nc.values_load_multi_w_load_instructions(
                                base_i[0:1, bass.ds(bl * GB, GB)], engines=(mybir.EngineType.DVE,),
                                min_val=0, max_val=N - 1,
                                skip_runtime_bounds_check_because="dst names nodes of the graph")[1]
                            for q in range(GB):
                                make_hot(l, bl * GB + q + AHEAD, (q + AHEAD) % GB)
                                k = m * GB + q - 2
                                if k >= 0:
                                    add_in(2 * i + k // GB, k % GB, base[k])
                                if q == 0:
                                    stage_indices(l, bl + 1, 1 - m)
                                if take and q == 0 and l == 0:
                                    clear(n, t)
                                if take and q:
                                    finish(l, n, m, m, 16 * (i - LAG // 2 + 1),
                                           None if first else 16 * (i - LAG // 2), (q,))
                        for k in (2 * GB - 2, 2 * GB - 1):
                            add_in(2 * i + 1, k % GB, base[k])

                    with dve.Fori(0, LAG // 2) as i:
                        body(i, False, False)
                    body(LAG // 2, True, True)
                    with dve.Fori(LAG // 2 + 1, BLOCKS // 2) as i:
                        body(i, True, False)
                    for late, step in ((0, 0), (0, 1), (1, 0), (1, 1), (0, 2), (0, 3), (1, 2), (2, 0), (2, 1), (1, 3),
                                       (2, 2), (2, 3)):
                        t = TILES - 3 + late
                        if step:
                            finish(l, l * TILES + t, t % 2, late, 16 if late == 2 else 16 * PAIRS,
                                   None if late == 2 else 16 * (PAIRS - 1), (step,))
                        elif l == 0:
                            clear(t, t)
            with dve.Else():
                for l in range(2):
                    dve.wait_ge(g_zero, 3 * l + 3)
                    with dve.Fori(0, CHUNKS) as c:
                        n = l * CHUNKS + c
                        LINKED = 6

                        def then(ins, k):
                            ins.then_inc(g_link, 1)
                            dve.wait_ge(g_link, LINKED * n + k)

                        node, weight = dstT[:, bass.ds(c, 1)], wT[:, bass.ds(c, 1)]
                        nc.vector.tensor_copy(dst_b, node.to_broadcast([P, P])).then_inc(g_dstb, 1)
                        dve.wait_ge(g_row, n + 1)
                        then(nc.vector.tensor_scalar(eq, ps[:, 1, 0:P], node, None, ALU.is_equal), 1)
                        then(nc.vector.tensor_tensor(dst_b, eq, below, ALU.mult), 2)
                        nc.vector.tensor_reduce(col[:, 0:1], dst_b, AX.X, ALU.add)
                        then(nc.vector.tensor_scalar(col[:, 1:2], node, float(N), None, ALU.is_lt), 3)
                        nc.vector.tensor_tensor(col[:, 2:3], node, trash, ALU.subtract)
                        then(nc.vector.tensor_scalar(col[:, 3:4], col[:, 0:1], 0.0, col[:, 1:2],
                                                     ALU.is_equal, ALU.mult), 4)
                        then(nc.vector.tensor_tensor(col[:, 4:5], col[:, 2:3], col[:, 3:4], ALU.mult), 5)
                        then(nc.vector.tensor_tensor(gen_to, col[:, 4:5], trash, ALU.add), 6)
                        dve.wait_ge(g_rows, 16 * n + 16)
                        nc.vector.tensor_tensor(ht[:, 0, :], rows[:, 0, 0:D], rows[:, 0, D:2 * D], ALU.add)
                        nc.vector.tensor_scalar(eqw, eq, weight, None, ALU.mult).then_inc(g_eq, 1)
                        dve.wait_ge(g_sum, n + 1)
                        dve.wait_ge(g_sc, 16 * n + 16)

                    for t in range(2):
                        finish(l, l * TILES + t, t, t, 16, None)
                    with dve.Fori(1, TILES // 2) as j:
                        for b in range(2):
                            finish(l, l * TILES + 2 * j + b, b, b, 16 * (j + 1), 16 * j)
                    finish(l, l * TILES + TILES - 1, 0, 2, 16, None)



_INS = ["x", "src", "dst", "edge_weight", "L0_gnn_weight", "L1_gnn_W", "L1_gnn_b"]


def kernel(**inputs):
    import concourse.bacc as _bacc
    from concourse.bass_utils import run_bass_kernel_spmd as _run

    nc = _bacc.Bacc("TRN2", target_bir_lowering=False, num_devices=1)
    arrays, args = {}, []
    for name in _INS:
        a = np.ascontiguousarray(inputs[name])
        arrays[f"in_{name}_dram"] = a
        args.append(nc.dram_tensor(f"in_{name}_dram", a.shape, mybir.dt.from_np(a.dtype), kind="ExternalInput").ap())
    shape = tuple(inputs["x"].shape)
    args.append(nc.dram_tensor("out_0_dram", shape, mybir.dt.float32, kind="ExternalOutput").ap())
    gnn_kernel(nc, *args)
    r = _run(nc, [arrays], core_ids=[0])
    return r.results[0]["out_0_dram"]
```

```python
import numpy as np
import concourse.bass as bass
from concourse import mybir
from contextlib import ExitStack


def gnn_kernel(nc, x, src, dst, edge_weight, w_first, w_second, bias, out):
    f32, bf16, f16, i32 = mybir.dt.float32, mybir.dt.bfloat16, mybir.dt.float16, mybir.dt.int32
    ALU = mybir.AluOpType
    ACT = mybir.ActivationFunctionType
    AX = mybir.AxisListType

    P = 128
    N, D = x.shape
    E = src.shape[0]
    KD = D // P
    TILES = -(-N // P)
    REST = N - (TILES - 1) * P
    REAL = -(-E // P)
    GC, GB = 4, 4
    BLOCK = GC * GB
    BLOCKS = 2 * -(-REAL // (2 * BLOCK))
    CHUNKS = BLOCKS * BLOCK
    GROUPS = BLOCKS * GB
    PADS = CHUNKS * P - E
    NAT = -(-REAL // P)
    WIN = 42
    LAG = 6
    LATE = TILES - (BLOCKS - LAG)
    COLS = TILES * P + WIN
    NOWHERE = float(1 << 20)
    SCALE = 2048.0
    EPS = 1e-5
    START = 8
    AHEAD = 3
    LN = 2
    XB = 4
    STEPS = (TILES - 1) // LN
    ROUNDS = STEPS // XB
    ZEROS = -(-COLS // (STEPS - XB))
    assert ROUNDS * XB == STEPS and ROUNDS == 6 and STEPS * LN == TILES - 1
    assert TILES % 2 and LATE == 3 and BLOCKS % 2 == 0 and LAG % 2 == 0

    ctx = ExitStack()
    with ctx:
        def sb(name, shape, dt):
            return ctx.enter_context(nc.sbuf_tensor(name, shape, dt))

        def sem(name):
            return ctx.enter_context(nc.semaphore(name))

        h_dram = [nc.dram_tensor(f"h{l}_dram", (N, 2 * D), f16, kind="Internal").ap() for l in range(2)]
        y_dram = nc.dram_tensor("y_dram", (N, D), f32, kind="Internal").ap()
        sum_dram = nc.dram_tensor("sum_dram", (N + P, D), f32, kind="Internal").ap()

        aggT = sb("aggT", [P, KD, COLS], f32)
        rows = sb("rows", [P, BLOCK, 2 * D], f16)
        idxT = sb("idxT", [P, CHUNKS + BLOCK], i32)
        dstT = sb("dstT", [P, CHUNKS], f32)
        wT = sb("wT", [P, CHUNKS], f32)
        relT = sb("relT", [P, CHUNKS + AHEAD * GC], bf16)
        w3 = sb("w3", [P, CHUNKS + AHEAD * GC, 3], bf16)
        idx_now = sb("idx_now", [P, 2, BLOCK], i32)
        wmat = sb("wmat", [P, 2, KD, D], f32)
        ident = sb("ident", [P, P], f32)
        fold = sb("fold", [P, WIN], f32)
        row0 = sb("row0", [P, P], f32)
        iota_w = sb("iota_w", [P, WIN], bf16)
        ones = sb("ones", [P, 1], f32)
        zero = sb("zero", [P, 1], f32)
        eps = sb("eps", [P, 1], f32)
        low = sb("low", [1, GROUPS], f32)
        base_i = sb("base_i", [1, GROUPS], i32)
        early = sb("early", [1, GROUPS], f32)
        counts = sb("counts", [P, 3], f32)
        flag_f = sb("flag_f", [1, 2], f32)
        flag_i = sb("flag_i", [1, 1], i32)
        stats = sb("stats", [P, XB, LN, 6], f32)
        mv = sb("mv", [P, XB, LN, 2], f32)
        std = sb("std", [P, XB, LN], f32)
        rstd = sb("rstd", [P, XB, LN], f32)
        shift = sb("shift", [P, XB, LN], f32)
        z = LN * D
        SCRATCH = (2 * XB + 1) * z
        scratch = sb("scratch", [P, SCRATCH], f32)

        ln_x = scratch[:, 0:XB * z].rearrange("p (b t d) -> p b t d", b=XB, t=LN)
        ln_pair = scratch[:, XB * z:2 * XB * z].bitcast(f16).rearrange("p (b t d) -> p b t d", b=XB, t=LN)
        ln_h = wmat[:, :, :, :].rearrange("p l k d -> p (l k d)").rearrange("p (b t d) -> p b t d", b=XB, t=LN)
        at = [0]

        def part(words):
            at[0] += words
            assert at[0] <= SCRATCH
            return scratch[:, at[0] - words:at[0]]

        hot3 = part(4 * GC * P // 2).bitcast(bf16).rearrange("p (b c m) -> p b c m", b=4, c=GC)
        hot = part(2 * GC * WIN // 2).bitcast(bf16).rearrange("p (b c j) -> p b c j", b=2, c=GC)
        xt = part(3 * D).rearrange("p (b d) -> p b d", b=3)
        ht = part(3 * D).rearrange("p (b d) -> p b d", b=3)
        pair_words = part(3 * D)
        pair = pair_words.bitcast(f16).rearrange("p (b d) -> p b d", b=3)
        out_t = pair_words.rearrange("p (b d) -> p b d", b=3)
        stage = part(2 * D).rearrange("p (b k n) -> p b k n", b=2, k=KD)
        agg = part(2 * D).rearrange("p (b d) -> p b d", b=2)
        bias_t = part(D)
        dst_b, eq, eqw, below = (part(P) for _ in range(4))
        col = part(8)
        trash = part(1)
        gen_idx, gen_to = (part(1).bitcast(i32) for _ in range(2))

        temp = rows[:, :, :].rearrange("p a b -> p (a b)").bitcast(f32)
        w_nat = NAT * P

        def table(k):
            return temp[:, k * w_nat:(k + 1) * w_nat].rearrange("p (g e) -> p g e", g=NAT)

        src_nat, dst_nat = table(0).bitcast(i32), table(1).bitcast(i32)
        nat_f = [table(2), table(3), table(4)]
        bases = temp[:, 5 * w_nat:5 * w_nat + GROUPS]
        rem = temp[:, 6 * w_nat:6 * w_nat + CHUNKS]
        junk = temp[:, 7 * w_nat:7 * w_nat + CHUNKS]

        ps = ctx.enter_context(nc.psum_tensor("ps", [P, 8, D], f32))
        turned = [ps[:, 2 * k:2 * k + 2, :].rearrange("p a b -> p (a b)") for k in range(3)]

        s_const = sem("constants_made")
        s_fill = sem("tables_filled")
        s_tab = sem("edge_tables_loaded")
        s_conv = sem("tables_as_float")
        s_turn = sem("tables_turned")
        s_dstT = sem("dst_table_ready")
        s_base = sem("bases_spread")
        s_bases = sem("bases_copied")
        s_rel = sem("rel_table_ready")
        s_idxT = sem("index_table_ready")
        s_wT = sem("weight_table_ready")
        s_w3 = sem("weight_parts")
        s_cnt = sem("counts_ready")
        s_tot = sem("totals_ready")
        s_flag = sem("flag_ready")
        s_link = sem("vector_chain")
        s_wld = sem("weights_loaded")
        s_zero = sem("sums_zeroed")
        s_lnx = [sem(f"ln_x_loaded{b}") for b in range(XB)]
        s_lnst = [sem(f"ln_pair_stored{b}") for b in range(XB)]
        s_lnbn = sem("ln_halves")
        s_lnrs = sem("ln_rstd")
        s_lnmv = sem("ln_moments")
        s_lnsd = sem("ln_std")
        s_lnsh = sem("ln_shift")
        s_lnh0 = sem("ln_h_first_tile")
        s_lnh1 = sem("ln_h_second_tile")
        s_lnhi = sem("ln_high_second_tile")
        s_lnlo0 = sem("ln_remainder_first_tile")
        s_lnlo1 = sem("ln_remainder_second_tile")
        s_index_go = sem("pool_may_gather")
        s_aggr_go = sem("vector_may_aggregate")
        s_idx = sem("indices_staged")
        s_rows = [sem(f"rows_gathered{b}") for b in range(GB)]
        s_hot = sem("onehot_made")
        s_hot3 = sem("weights_in_place")
        s_sum = sem("group_summed")
        s_evac = sem("sum_copied")
        s_fold = sem("group_folded")
        s_add = sem("group_added")
        s_stage = sem("tile_staged")
        s_proj = sem("tile_projected")
        s_x1 = sem("residual_added")
        s_bn = sem("tile_halves")
        s_mv = sem("tile_moments")
        s_rstd = sem("tile_rstd")
        s_std = sem("tile_std")
        s_shift = sem("tile_shift")
        s_h = sem("tile_h")
        s_lo = sem("tile_pair_ready")
        s_pair = sem("tile_finished")
        s_out = sem("tile_out")
        s_ld = [[sem(f"tile_loaded{l}{b}") for b in range(3)] for l in range(2)]
        s_hst = [sem(f"h_stored{b}") for b in range(3)]
        s_yst = [sem(f"y_stored{b}") for b in range(3)]
        s_ost = [sem(f"out_stored{b}") for b in range(3)]
        g_link = sem("g_vector_chain")
        g_zero = sem("g_zero_tile")
        g_ones = sem("g_ones_made")
        g_zst = sem("g_sums_cleared")
        g_idx = sem("g_index_copied")
        g_rows = sem("g_rows_gathered")
        g_dstb = sem("g_dst_spread")
        g_row = sem("g_dst_row")
        g_eq = sem("g_matrix_ready")
        g_sum = sem("g_chunk_summed")
        g_msg = sem("g_chunk_copied")
        g_sc = sem("g_chunk_added")
        g_ld = sem("g_tile_loaded")
        g_tr = sem("g_tile_turned")

        block = ctx.enter_context(nc.Block())
        wm = [w_first, w_second]
        PAIRS = TILES // 2

        def stored_all(b):
            return 16 * (1 if b == 2 else PAIRS)

        def ln_stored_all(b):
            return 16 * (ROUNDS + (b == 0))

        def whole(t):
            return t * P, (REST if isinstance(t, int) and t == TILES - 1 else P)

        def node_rows(ap, t):
            n0, n = whole(t)
            return ap[bass.ds(n0, n), :]

        @block.sync
        def _(sp):
            xg = x[0:STEPS * LN * P, :].rearrange("(s t p) d -> s p t d", t=LN, p=P)
            hg = h_dram[0][0:STEPS * LN * P, :].rearrange("(s t p) d -> s p t d", t=LN, p=P)

            def step_of(ap, step):
                return ap[step] if isinstance(step, int) else ap[bass.ds(step, 1)].rearrange("s p t d -> (s p) t d")

            def ln_load(step, b):
                sp.dma_start(ln_x[:, b], step_of(xg, step)).then_inc(s_lnx[b], 16)

            def ln_store(step, b):
                sp.wait_ge(s_lnlo0, step + 1)
                sp.wait_ge(s_lnlo1, step + 1)
                sp.dma_start(step_of(hg, step), ln_pair[:, b]).then_inc(s_lnst[b], 16)

            for b in range(XB):
                ln_load(b, b)
            sp.wait_ge(s_fill, 1)
            full = (NAT - 1) * P * P
            more = (E - full) // P
            for nat, edges in ((dst_nat, dst), (src_nat, src), (nat_f[0], edge_weight)):
                sp.dma_start(nat[:, 0:NAT - 1, :], edges[0:full].rearrange("(g p e) -> p g e", p=P, e=P)
                             ).then_inc(s_tab, 16)
                sp.dma_start(nat[0:more, NAT - 1, :], edges[full:full + more * P].rearrange("(p e) -> p e", e=P)
                             ).then_inc(s_tab, 16)
                sp.dma_start(nat[more:more + 1, NAT - 1, 0:E - full - more * P],
                             edges[full + more * P:E].rearrange("(p e) -> p e", p=1)).then_inc(s_tab, 16)
            with sp.Fori(0, ROUNDS - 1) as j:
                for b in range(XB):
                    sp.wait_ge(s_lnh1, XB * j + b + 1)
                    ln_load(XB * (j + 1) + b, b)
                    ln_store(XB * j + b, b)
            sp.wait_ge(s_lnh1, STEPS - XB + 1)
            sp.dma_start(ln_x[0:REST, 0, 0, :], x[N - REST:N, :]).then_inc(s_lnx[0], 16)
            for b in range(XB):
                ln_store(STEPS - XB + b, b)
            sp.wait_ge(s_lnlo0, STEPS + 1)
            sp.dma_start(h_dram[0][N - REST:N, :], ln_pair[0:REST, 0, 0, :]).then_inc(s_lnst[0], 16)
            for l in range(2):
                sp.dma_start(wmat[:, l], wm[l].rearrange("(k p) d -> p k d", p=P)).then_inc(s_wld, 16)
            for b in range(XB):
                sp.wait_ge(s_lnst[b], ln_stored_all(b))

            def load(l, t, b):
                n0, n = whole(t)
                sp.dma_start(xt[0:n, b, :], node_rows(x if l == 0 else y_dram, t)).then_inc(s_ld[l][b], 16)

            def store_h(t, b):
                n0, n = whole(t)
                sp.wait_ge(s_lo, t + 1)
                sp.dma_start(node_rows(h_dram[1], t), pair[0:n, b, :]).then_inc(s_hst[b], 16)

            def store_y(t, b):
                n0, n = whole(t)
                sp.wait_ge(s_pair, START + t + 1)
                sp.dma_start(node_rows(y_dram, t), xt[0:n, b, :]).then_inc(s_yst[b], 16)

            def store_second(t, b):
                n0, n = whole(t)
                sp.wait_ge(s_out, t + 1)
                sp.dma_start(node_rows(out, t), out_t[0:n, b, :]).then_inc(s_ost[b], 16)

            for l in range(2):
                load(l, 0, 0)
                load(l, 1, 1)
                load(l, TILES - 1, 2)
                if l == 0:
                    sp.dma_start(bias_t, bias.rearrange("(a d) -> a d", a=1).to_broadcast([P, D])).then_inc(s_wld, 16)
                with sp.Fori(0, PAIRS - 1) as j:
                    for b in range(2):
                        if l == 0:
                            store_h(2 * j + b, b)
                            store_y(2 * j + b, b)
                            sp.wait_ge(s_yst[b], 16 * (j + 1))
                        else:
                            store_second(2 * j + b, b)
                        load(l, 2 * j + b + 2, b)
                late = (TILES - 3, TILES - 2, TILES - 1)
                if l == 0:
                    store_h(late[0], 0)
                    store_y(late[0], 0)
                    store_h(late[1], 1)
                    store_h(late[2], 2)
                    store_y(late[1], 1)
                    store_y(late[2], 2)
                else:
                    for b in range(3):
                        store_second(late[b], b)
                for b in range(3):
                    if l == 0:
                        sp.wait_ge(s_hst[b], stored_all(b))
                        sp.wait_ge(s_yst[b], stored_all(b))
                    else:
                        sp.wait_ge(s_ost[b], stored_all(b))

        @block.gpsimd
        def _(pool):
            nc.gpsimd.memset(ident[:, :], 0.0).then_inc(s_const, 1)
            nc.gpsimd.memset(fold[:, :], 0.0).then_inc(s_const, 1)
            nc.gpsimd.memset(row0[:, :], 0.0).then_inc(s_const, 1)
            pool.wait_ge(s_const, 3)
            nc.gpsimd.affine_select(out=ident[:, :], in_=ident[:, :], compare_op=ALU.not_equal, fill=1.0,
                                    base=0, pattern=[[-1, P]], channel_multiplier=1).then_inc(s_const, 1)
            for k in range(3):
                nc.gpsimd.affine_select(out=fold[:, :], in_=fold[:, :], compare_op=ALU.not_equal,
                                        fill=1.0 / SCALE, base=-k * WIN, pattern=[[-1, WIN]],
                                        channel_multiplier=1).then_inc(s_const, 1)
                pool.wait_ge(s_const, 5 + k)
            nc.gpsimd.affine_select(out=row0[:, :], in_=row0[:, :], compare_op=ALU.not_equal, fill=1.0,
                                    base=0, pattern=[[0, P]], channel_multiplier=1).then_inc(s_const, 1)
            nc.gpsimd.iota(iota_w[:, :], pattern=[[1, WIN]], base=0, channel_multiplier=0,
                           allow_small_or_imprecise_dtypes=True).then_inc(s_const, 1)
            nc.gpsimd.iota(low[:, :], pattern=[[P, BLOCKS], [0, GB]], base=-(LAG - 2) * P, channel_multiplier=0,
                           allow_small_or_imprecise_dtypes=True).then_inc(s_const, 1)

            def ln_rest(b, k):
                pool.wait_ge(s_lnhi, k + 1)
                nc.gpsimd.tensor_tensor(ln_pair[:, b, 1, D:2 * D], ln_h[:, b, 1, :], ln_pair[:, b, 1, 0:D],
                                        ALU.subtract).then_inc(s_lnlo1, 1)

            def table_dst():
                pool.wait_ge(s_tab, 9 * 16)
                nc.gpsimd.tensor_copy(nat_f[1], dst_nat).then_inc(s_conv, 1)

            def table_src():
                nc.gpsimd.tensor_copy(nat_f[2], src_nat).then_inc(s_conv, 1)

            def weight_rest(k):
                pool.wait_ge(s_w3, 2 * k + 1)
                nc.gpsimd.tensor_tensor(rem, wT[:, :] if k == 0 else rem, w3[:, 0:CHUNKS, k], ALU.subtract
                                        ).then_inc(s_w3, 1)

            def table_rel():
                pool.wait_ge(s_bases, 1)
                nc.gpsimd.tensor_tensor(relT[:, 0:CHUNKS].rearrange("p (g c) -> p g c", c=GC),
                                        dstT[:, :].rearrange("p (g c) -> p g c", c=GC),
                                        bases.unsqueeze(2).to_broadcast([P, GROUPS, GC]),
                                        ALU.subtract).then_inc(s_rel, 1)

            def zeros(j, b, n=ZEROS):
                c = (XB * (j - 1) + b) * ZEROS
                nc.gpsimd.memset(aggT[:, :, c:c + n], 0.0).then_inc(s_zero, 1)

            for b in range(XB):
                ln_rest(b, b)
                if b == 2:
                    table_dst()
                if b == 3:
                    table_src()
            for j in range(1, ROUNDS - 1):
                for b in range(XB):
                    ln_rest(b, XB * j + b)
                    if (j, b) == (1, 3):
                        weight_rest(0)
                    if (j, b) == (2, 0):
                        table_rel()
                    if (j, b) == (2, 2):
                        weight_rest(1)
                    zeros(j, b)
            for b in range(XB):
                ln_rest(b, XB * (ROUNDS - 1) + b)
                zeros(ROUNDS - 1, b, ZEROS if b < XB - 1 else COLS - (STEPS - XB - 1) * ZEROS)

            pool.wait_ge(s_flag, 1)
            flag = pool.value_load(flag_i[0:1, 0:1], min_val=0, max_val=1)
            pool.wait_ge(s_w3, 6)

            def h_ready(l):
                if l == 0:
                    for b in range(XB):
                        pool.wait_ge(s_lnst[b], ln_stored_all(b))
                else:
                    for b in range(3):
                        pool.wait_ge(s_hst[b], stored_all(b))

            def before_indexed():
                pool.sem_inc(s_index_go, 1)

            with pool.If(flag == 1):
                for l in range(2):
                    h_ready(l)
                    with pool.Fori(0, BLOCKS // 2) as i:
                        for m in range(2):
                            bl = 2 * i + m
                            pool.wait_ge(s_idx, l * BLOCKS + bl + 1)
                            for q in range(GB):
                                g = l * GROUPS + bl * GB + q
                                pool.wait_ge(s_sum, START + g + 1 - GB)
                                before_indexed()
                                for c in range(GC):
                                    k = q * GC + c
                                    pool.indirect_dma_start(
                                        out=rows[:, k, :], out_offset=None, in_=h_dram[l][:, :],
                                        in_offset=bass.IndirectOffsetOnAxis(ap=idx_now[:, m, k:k + 1], axis=0),
                                    ).then_inc(s_rows[q], 16)
            with pool.Else():
                for l in range(2):
                    h_ready(l)
                    if l == 1:
                        pool.wait_ge(g_ld, 16 * TILES)
                    nc.gpsimd.memset(agg[:, 0, :], 0.0).then_inc(g_zero, 1)
                    nc.gpsimd.memset(below, 1.0).then_inc(g_ones, 1)
                    pool.wait_ge(g_ones, l + 1)
                    nc.gpsimd.affine_select(out=below, in_=below, compare_op=ALU.is_gt, fill=0.0, base=0,
                                            pattern=[[-1, P]], channel_multiplier=1).then_inc(g_zero, 1)
                    nc.gpsimd.iota(trash, pattern=[[0, 1]], base=N, channel_multiplier=1,
                                   allow_small_or_imprecise_dtypes=True).then_inc(g_zero, 1)
                    pool.wait_ge(g_zero, 3 * l + 3)
                    with pool.Fori(0, TILES) as t:
                        pool.dma_start(sum_dram[bass.ds(t * P, P), :], agg[:, 0, :]).then_inc(g_zst, 16)
                    pool.dma_start(sum_dram[TILES * P:N + P, :], agg[0:N + P - TILES * P, 0, :]).then_inc(g_zst, 16)
                    pool.wait_ge(g_zst, 16 * (TILES + 1) * (l + 1))
                    with pool.Fori(0, CHUNKS) as c:
                        n = l * CHUNKS + c
                        nc.gpsimd.tensor_copy(gen_idx, idxT[:, bass.ds(c, 1)]).then_inc(g_idx, 1)
                        pool.wait_ge(g_idx, n + 1)
                        before_indexed()
                        pool.indirect_dma_start(
                            out=rows[:, 0, :], out_offset=None, in_=h_dram[l][:, :],
                            in_offset=bass.IndirectOffsetOnAxis(ap=gen_idx, axis=0)).then_inc(g_rows, 16)
                        pool.wait_ge(g_msg, n + 1)
                        before_indexed()
                        pool.indirect_dma_start(
                            out=sum_dram[:, :], out_offset=bass.IndirectOffsetOnAxis(ap=gen_to, axis=0),
                            in_=agg[:, 1, :], in_offset=None, compute_op=ALU.add).then_inc(g_sc, 16)
                        pool.wait_ge(g_sc, 16 * n + 16)

        @block.scalar
        def _(act):
            def ln_std(b, n, t=LN):
                act.wait_ge(s_lnmv, n)
                act.activation(std[:, b, 0:t], mv[:, b, 0:t, 1], ACT.Sqrt, bias=eps[:, :],
                               scale=1.0 / SCALE ** 2).then_inc(s_lnsd, 1)

            def ln_relu(b, k, stored, t=LN):
                act.wait_ge(s_lnsh, k + 1)
                if stored is not None:
                    act.wait_ge(s_lnst[b], stored)
                for i, o, done in ((0, ln_h[:, b, 0, :], None), (0, ln_pair[:, b, 0, 0:D], s_lnh0),
                                   (1, ln_h[:, b, 1, :], s_lnh1)):
                    if i < t:
                        ins = act.activation(o, ln_x[:, b, i, :], ACT.Relu,
                                             bias=shift[:, b, i:i + 1], scale=rstd[:, b, i:i + 1])
                        if done is not None:
                            ins.then_inc(done, 1)

            def table_copy(to, k, done):
                act.wait_ge(s_turn, k + 1)
                act.activation(to, turned[k][:, 0:CHUNKS], ACT.Copy).then_inc(done, 1)

            def table_bases():
                act.wait_ge(s_base, 1)
                act.activation(bases, ps[:, 6, 0:GROUPS], ACT.Copy).then_inc(s_bases, 1)

            def weight_part(k):
                if k == 0:
                    act.wait_ge(s_wT, 1)
                else:
                    act.wait_ge(s_w3, 2 * k)
                act.activation(w3[:, 0:CHUNKS, k], rem if k else wT[:, :], ACT.Copy).then_inc(s_w3, 1)

            def ln_step(j, b, first=False, last=False):
                k = XB * j + b
                ln_relu(b, k, None if first else 16 * j)
                ln_std((b + 1) % XB, k + 2, 1 if last and b == XB - 1 else LN)

            ln_std(0, 1)
            for b in range(XB):
                ln_step(0, b, first=True)
            ln_step(1, 0)
            table_copy(wT[:, :], 0, s_wT)
            ln_step(1, 1)
            weight_part(0)
            ln_step(1, 2)
            table_copy(dstT[:, :], 1, s_dstT)
            ln_step(1, 3)
            table_copy(idxT[:, 0:CHUNKS], 2, s_idxT)
            ln_step(2, 0)
            table_bases()
            ln_step(2, 1)
            ln_step(2, 2)
            weight_part(1)
            ln_step(2, 3)
            ln_step(3, 0)
            weight_part(2)
            for b in range(1, XB):
                ln_step(3, b)
            with act.Fori(4, ROUNDS - 1) as j:
                for b in range(XB):
                    ln_step(j, b)
            for b in range(XB):
                ln_step(ROUNDS - 1, b, last=True)
            ln_relu(0, STEPS, 16 * ROUNDS, 1)

            act.wait_ge(s_flag, 1)
            flag = act.value_load(flag_i[0:1, 0:1], min_val=0, max_val=1)

            def stage_tile(n, b, t, added):
                act.wait_ge(s_add, added)
                act.wait_ge(s_proj, START + n - 1)
                act.activation(stage[:, b], aggT[:, :, bass.ds(t * P, P)], ACT.Copy).then_inc(s_stage, 1)

            def clear(t, tiles=1):
                act.activation(aggT[:, :, bass.ds(t * P, tiles * P)],
                               zero[:, :].unsqueeze(2).to_broadcast([P, KD, tiles * P]), ACT.Copy)

            def std_tile(n, b):
                act.wait_ge(s_mv, n + 1)
                act.activation(std[:, b, 0:1], mv[:, b, 0, 1:2], ACT.Sqrt, bias=eps[:, :],
                               scale=1.0 / SCALE ** 2).then_inc(s_std, 1)

            def relu_tile(n, b, stored):
                act.wait_ge(s_shift, n + 1)
                act.wait_ge(s_pair, START + n - 1)
                if stored is not None:
                    act.wait_ge(s_hst[b], stored)
                act.activation(ht[:, b, :], xt[:, b, :], ACT.Relu, bias=shift[:, b, 0:1], scale=rstd[:, b, 0:1])
                act.activation(pair[:, b, 0:D], xt[:, b, :], ACT.Relu, bias=shift[:, b, 0:1],
                               scale=rstd[:, b, 0:1]).then_inc(s_h, 1)

            act.sem_inc(s_evac, START)
            with act.If(flag == 1):
                for l in range(2):
                    def body(i, take=True, first=False, last=False):
                        for m in range(2):
                            bl = 2 * i + m
                            t = bl - LAG
                            n = l * TILES + t
                            if take and not (last and m):
                                stage_tile(n, m, t, START + l * GROUPS + GB * (bl - 1))
                            for q in range(GB):
                                g = l * GROUPS + bl * GB + q
                                act.wait_ge(s_sum, START + g + 1)
                                act.wait_ge(s_fold, START + g - 1)
                                act.activation(agg[:, q % 2, :], ps[:, q, :], ACT.Copy).then_inc(s_evac, 1)
                                if take and l == 0 and q == (0 if last and m else 1):
                                    std_tile(n, m)
                                    if not (last and m):
                                        clear(t)
                                if take and l == 0 and q == (1 if last and m else 2):
                                    relu_tile(n, m, None if first else 16 * (i - LAG // 2))
                                if last and (m, q) in ((0, 2), (1, 0)):
                                    stage_tile(n + 1, 1 - m, t + 1, START + l * GROUPS + GB * bl)

                    with act.Fori(0, LAG // 2) as i:
                        body(i, take=False)
                    body(LAG // 2, first=True)
                    with act.Fori(LAG // 2 + 1, BLOCKS // 2 - 1) as i:
                        body(i)
                    body(BLOCKS // 2 - 1, last=True)
                    n, t = l * TILES + TILES - 3, TILES - 3
                    if l == 0:
                        std_tile(n, 0)
                    act.sem_inc(s_stage, 2)
                    if l == 0:
                        relu_tile(n, 0, 16 * (PAIRS - 1))
                        std_tile(n + 1, 1)
                        relu_tile(n + 1, 1, 16 * (PAIRS - 1))
                        std_tile(n + 2, 2)
                        relu_tile(n + 2, 2, None)
                        clear(TILES - 4, 4)
            with act.Else():
                for l in range(2):
                    with act.Fori(0, CHUNKS) as c:
                        n = l * CHUNKS + c
                        act.wait_ge(g_sum, n + 1)
                        act.activation(agg[:, 1, :], ps[:, 0, :], ACT.Copy, scale=1.0 / SCALE).then_inc(g_msg, 1)

                    def gen_tile(t, b, stored, buf=None):
                        n = l * TILES + t
                        buf = b if buf is None else buf
                        act.dma_start(agg[:, 0, :], sum_dram[bass.ds(t * P, P), :]).then_inc(g_ld, 16)
                        act.wait_ge(g_tr, n + 1)
                        act.wait_ge(s_proj, START + n - 1)
                        act.activation(stage[:, b], ps[:, 4, :].rearrange("p (k n) -> p k n", k=KD), ACT.Copy
                                       ).then_inc(s_stage, 1)
                        if l == 0:
                            std_tile(n, buf)
                            relu_tile(n, buf, stored)

                    act.wait_ge(g_sc, 16 * CHUNKS * (l + 1))
                    for b in range(2):
                        gen_tile(b, b, None)
                    with act.Fori(1, TILES // 2) as j:
                        for b in range(2):
                            gen_tile(2 * j + b, b, 16 * j)
                    gen_tile(TILES - 1, 0, None, 2)

        @block.tensor
        def _(pe):
            pe.wait_ge(s_const, 4)
            for k in range(3):
                if k == 0:
                    pe.wait_ge(s_tab, 9 * 16)
                else:
                    pe.wait_ge(s_conv, k)
                for g in range(NAT):
                    last = nc.tensor.transpose(turned[k][:, g * P:(g + 1) * P], nat_f[k][:, g, :], ident[:, :])
                last.then_inc(s_turn, 1)
            pe.wait_ge(s_const, 8)
            pe.wait_ge(s_dstT, 1)
            nc.tensor.matmul(ps[:, 6, 0:GROUPS], row0[:, :], dstT[:, ::GC], start=True, stop=True).then_inc(s_base, 1)
            pe.wait_ge(s_cnt, 1)
            nc.tensor.matmul(ps[0:1, 7, 0:3], ones[:, :], counts[:, :], start=True, stop=True).then_inc(s_tot, 1)

            pe.wait_ge(s_flag, 1)
            flag = pe.value_load(flag_i[0:1, 0:1], min_val=0, max_val=1)
            pe.sem_inc(s_sum, START)
            pe.sem_inc(s_fold, START)
            pe.sem_inc(s_proj, START)

            def product(l, b, sums):
                pe.wait_ge(s_wld, 48)
                for k in range(KD):
                    last = nc.tensor.matmul(ps[:, 6 + b, :], sums(k), wmat[:, l, k, :],
                                            start=(k == 0), stop=(k == KD - 1))
                last.then_inc(s_proj, 1)

            def project(l, n, b):
                pe.wait_ge(s_stage, n + 1)
                pe.wait_ge(s_x1, START + n - 1)
                product(l, b, lambda k: stage[:, b, k, :])

            with pe.If(flag == 1):
                for l in range(2):
                    def add_up(bl, q):
                        g = l * GROUPS + bl * GB + q
                        pe.wait_ge(s_rows[q], 16 * GC * (l * BLOCKS + bl + 1))
                        pe.wait_ge(s_hot3, START + g + 1)
                        pe.wait_ge(s_evac, START + g + 1 - GB)
                        for c in range(GC):
                            for part_ in range(2):
                                last = nc.tensor.matmul(
                                    ps[:, q, :], hot3[:, q, c, :],
                                    rows[:, q * GC + c, part_ * D:(part_ + 1) * D],
                                    start=(c == 0 and part_ == 0), stop=(c == GC - 1 and part_ == 1))
                        last.then_inc(s_sum, 1)

                    def fold_up(bl, q):
                        g = l * GROUPS + bl * GB + q
                        pe.wait_ge(s_evac, START + g + 1)
                        pe.wait_ge(s_add, START + g - 1)
                        for k in range(KD):
                            last = nc.tensor.matmul(ps[:, 4 + q % 2, k * WIN:(k + 1) * WIN],
                                                    agg[:, q % 2, k * P:(k + 1) * P], fold[:, :],
                                                    start=True, stop=True)
                        last.then_inc(s_fold, 1)

                    def body(i, take=True, last=False):
                        for m in range(2):
                            bl = 2 * i + m
                            for q in range(GB):
                                add_up(bl, q)
                                if q or m:
                                    fold_up(bl if q else bl - 1, (q - 1) % GB)
                                if take and q == 1 and not (last and m):
                                    project(l, l * TILES + bl - LAG, m)
                                if last and (m, q) in ((0, 3), (1, 1)):
                                    project(l, l * TILES + bl - LAG + 1, 1 - m)
                        fold_up(2 * i + 1, GB - 1)

                    with pe.Fori(0, LAG // 2) as i:
                        body(i, take=False)
                    with pe.Fori(LAG // 2, BLOCKS // 2 - 1) as i:
                        body(i)
                    body(BLOCKS // 2 - 1, last=True)
                    for t in (TILES - 2, TILES - 1):
                        pe.wait_ge(s_add, START + (l + 1) * GROUPS)
                        pe.wait_ge(s_x1, START + l * TILES + t - 1)
                        product(l, t % 2, lambda k: aggT[:, k, t * P:(t + 1) * P])
            with pe.Else():
                for l in range(2):
                    with pe.Fori(0, CHUNKS) as c:
                        n = l * CHUNKS + c
                        pe.wait_ge(g_dstb, n + 1)
                        nc.tensor.matmul(ps[:, 1, 0:P], dst_b, ident[:, :], start=True, stop=True).then_inc(g_row, 1)
                        pe.wait_ge(g_eq, n + 1)
                        nc.tensor.matmul(ps[:, 0, :], eqw, ht[:, 0, :], start=True, stop=True).then_inc(g_sum, 1)

                    def gen_tile(t, b):
                        n = l * TILES + t
                        pe.wait_ge(g_ld, 16 * (n + 1))
                        for k in range(KD):
                            last = nc.tensor.transpose(ps[:, 4, k * P:(k + 1) * P], agg[:, 0, k * P:(k + 1) * P],
                                                       ident[:, :])
                        last.then_inc(g_tr, 1)
                        project(l, n, b)

                    with pe.Fori(0, TILES // 2) as j:
                        for b in range(2):
                            gen_tile(2 * j + b, b)
                    gen_tile(TILES - 1, 0)

        @block.vector
        def _(dve):
            nc.vector.memset(src_nat[:, NAT - 1, :], 0)
            nc.vector.memset(dst_nat[:, NAT - 1, :], int(NOWHERE))
            nc.vector.memset(nat_f[0][:, NAT - 1, :], 0.0).then_inc(s_fill, 1)
            nc.vector.memset(counts[:, :], 0.0)
            nc.vector.memset(ones[:, :], 1.0)
            nc.vector.memset(zero[:, :], 0.0)
            nc.vector.memset(eps[:, :], EPS / SCALE ** 2)
            chain = [0]

            def link(ins):
                chain[0] += 1
                ins.then_inc(s_link, 1)
                dve.wait_ge(s_link, chain[0])

            def ln_moments(b, k, loaded, t=LN):
                dve.wait_ge(s_lnx[b], loaded)
                for i in range(t):
                    last = nc.vector.bn_stats(stats[:, b, i, :], ln_x[:, b, i, :])
                last.then_inc(s_lnbn, 1)
                dve.wait_ge(s_lnbn, k + 1)
                dve.sem_inc(s_aggr_go, 1)
                for i in range(t):
                    last = nc.vector.bn_aggr(mv[:, b, i, :], stats[:, b, i, :])
                last.then_inc(s_lnmv, 1)

            def ln_shift(b, k, t=LN):
                dve.wait_ge(s_lnsd, k + 1)
                nc.vector.reciprocal(rstd[:, b, 0:t], std[:, b, 0:t]).then_inc(s_lnrs, 1)
                dve.wait_ge(s_lnrs, k + 1)
                nc.vector.scalar_tensor_tensor(out=shift[:, b, 0:t], in0=mv[:, b, 0:t, 0], scalar=-1.0,
                                               in1=rstd[:, b, 0:t], op0=ALU.mult, op1=ALU.mult).then_inc(s_lnsh, 1)

            def ln_rest(b, k):
                dve.wait_ge(s_lnh0, k + 1)
                nc.vector.tensor_tensor(ln_pair[:, b, 0, D:2 * D], ln_h[:, b, 0, :], ln_pair[:, b, 0, 0:D],
                                        ALU.subtract).then_inc(s_lnlo0, 1)

            def ln_high(b, k):
                dve.wait_ge(s_lnh1, k + 1)
                nc.vector.tensor_copy(ln_pair[:, b, 1, 0:D], ln_h[:, b, 1, :]).then_inc(s_lnhi, 1)

            def ahead_again():
                dve.wait_ge(s_idxT, 1)
                nc.vector.tensor_copy(idxT[:, CHUNKS:CHUNKS + BLOCK], idxT[:, 0:BLOCK])
                dve.wait_ge(s_rel, 1)
                nc.vector.tensor_copy(relT[:, CHUNKS:CHUNKS + AHEAD * GC], relT[:, 0:AHEAD * GC])
                dve.wait_ge(s_w3, 5)
                nc.vector.tensor_copy(w3[:, CHUNKS:CHUNKS + AHEAD * GC, :], w3[:, 0:AHEAD * GC, :]).then_inc(s_w3, 1)
                nc.vector.tensor_copy(base_i[:, :], ps[0:1, 6, 0:GROUPS])

            def count(k, bound, compare):
                dve.wait_ge(s_rel, 1)
                link(nc.vector.tensor_scalar(junk, relT[:, 0:CHUNKS], bound, 0.0, compare, ALU.add,
                                             accum_out=counts[:, k:k + 1]))

            def count_late():
                dve.wait_ge(s_const, 10)
                link(nc.vector.tensor_tensor(early[:, :], ps[0:1, 6, 0:GROUPS], low[:, :], ALU.is_lt))
                nc.vector.tensor_reduce(counts[0:1, 2:3], early[:, :], AX.X, ALU.add).then_inc(s_cnt, 1)

            def make_flag():
                dve.wait_ge(s_tot, 1)
                link(nc.vector.tensor_scalar(flag_f[:, 1:2], ps[0:1, 7, 2:3], float(P * CHUNKS), None, ALU.mult))
                link(nc.vector.tensor_scalar(flag_f[:, 0:1], ps[0:1, 7, 0:1], flag_f[:, 1:2], None, ALU.add))
                link(nc.vector.tensor_scalar(flag_f[:, 1:2], flag_f[:, 0:1], ps[0:1, 7, 1:2], float(PADS),
                                             ALU.add, ALU.is_equal))
                nc.vector.tensor_copy(flag_i[:, :], flag_f[:, 1:2]).then_inc(s_flag, 1)

            def ln_step(j, b, last=False):
                k = XB * j + b
                tiles = 1 if last and b == XB - 1 else LN
                ln_moments((b + 1) % XB, k + 1, 16 * (j + 1 + (b + 1) // XB), tiles)
                ln_rest(b, k)
                ln_shift((b + 1) % XB, k + 1, tiles)
                ln_high(b, k)

            ln_moments(0, 0, 16)
            ln_shift(0, 0)
            with dve.Fori(0, 3) as j:
                for b in range(XB):
                    ln_step(j, b)
            ln_step(3, 0)
            count(0, float(WIN), ALU.is_ge)
            ln_step(3, 1)
            count(1, 0.0, ALU.is_lt)
            ln_step(3, 2)
            count_late()
            ln_step(3, 3)
            ahead_again()
            for b in range(XB):
                ln_step(4, b)
            make_flag()
            for b in range(XB):
                ln_step(ROUNDS - 1, b, last=True)
            ln_rest(0, STEPS)

            link(nc.vector.memset(hot3[:, :, :, :], 0.0))
            flag = dve.value_load(flag_i[0:1, 0:1], min_val=0, max_val=1)
            dve.sem_inc(s_hot3, START)
            dve.sem_inc(s_add, START)
            dve.sem_inc(s_x1, START)
            dve.sem_inc(s_pair, START)

            def finish_first(n, b, buf, loaded, step):
                if step == 1:
                    dve.wait_ge(s_proj, START + n + 1)
                    dve.wait_ge(s_ld[0][buf], loaded)
                    nc.vector.tensor_tensor(xt[:, buf, :], xt[:, buf, :], ps[:, 6 + b, :], ALU.add).then_inc(s_x1, 1)
                    dve.wait_ge(s_x1, START + n + 1)
                    nc.vector.bn_stats(stats[:, buf, 0, :], xt[:, buf, :]).then_inc(s_bn, 1)
                    dve.wait_ge(s_bn, n + 1)
                    dve.sem_inc(s_aggr_go, 1)
                    nc.vector.bn_aggr(mv[:, buf, 0, :], stats[:, buf, 0, :]).then_inc(s_mv, 1)
                if step == 2:
                    dve.wait_ge(s_std, n + 1)
                    nc.vector.reciprocal(rstd[:, buf, 0:1], std[:, buf, 0:1]).then_inc(s_rstd, 1)
                    dve.wait_ge(s_rstd, n + 1)
                    nc.vector.scalar_tensor_tensor(out=shift[:, buf, 0:1], in0=mv[:, buf, 0, 0:1], scalar=-1.0,
                                                   in1=rstd[:, buf, 0:1], op0=ALU.mult, op1=ALU.mult
                                                   ).then_inc(s_shift, 1)
                if step == 3:
                    dve.wait_ge(s_h, n + 1)
                    nc.vector.tensor_tensor(pair[:, buf, D:2 * D], ht[:, buf, :], pair[:, buf, 0:D],
                                            ALU.subtract).then_inc(s_lo, 1)
                    nc.vector.scalar_tensor_tensor(out=xt[:, buf, :], in0=ht[:, buf, :], scalar=1.0 / SCALE,
                                                   in1=xt[:, buf, :], op0=ALU.mult, op1=ALU.add).then_inc(s_pair, 1)

            def finish_second(n, b, buf, loaded, stored, step):
                if step == 1:
                    dve.wait_ge(s_proj, START + n + 1)
                    dve.wait_ge(s_wld, 48)
                    nc.vector.tensor_tensor(ht[:, buf, :], ps[:, 6 + b, :], bias_t, ALU.add).then_inc(s_x1, 1)
                if step == 2:
                    dve.wait_ge(s_x1, START + n + 1)
                    dve.wait_ge(s_ld[1][buf], loaded)
                    if stored is not None:
                        dve.wait_ge(s_ost[buf], stored)
                    nc.vector.scalar_tensor_tensor(out=out_t[:, buf, :], in0=ht[:, buf, :], scalar=0.0,
                                                   in1=xt[:, buf, :], op0=ALU.max, op1=ALU.add).then_inc(s_out, 1)

            def finish(l, n, b, buf, loaded, stored, steps=(1, 2, 3)):
                for step in steps:
                    if l == 0:
                        finish_first(n, b, buf, loaded, step)
                    else:
                        finish_second(n, b, buf, loaded, stored, step)

            def make_hot(l, group, q):
                g, c = l * GROUPS + group, group * GC
                nc.vector.tensor_tensor(hot[:, q % 2], iota_w[:, :].unsqueeze(1).to_broadcast([P, GC, WIN]),
                                        relT[:, bass.ds(c, GC)].unsqueeze(2).to_broadcast([P, GC, WIN]),
                                        ALU.is_equal).then_inc(s_hot, 1)
                dve.wait_ge(s_hot, g + 1)
                dve.wait_ge(s_sum, START + g + 1 - GB)
                nc.vector.tensor_tensor(
                    hot3[:, q, :, 0:3 * WIN].rearrange("p c (a j) -> p c a j", a=3),
                    hot[:, q % 2].unsqueeze(2).to_broadcast([P, GC, 3, WIN]),
                    w3[:, bass.ds(c, GC), :].unsqueeze(3).to_broadcast([P, GC, 3, WIN]),
                    ALU.mult).then_inc(s_hot3, 1)

            def stage_indices(l, bl, b):
                nc.vector.tensor_copy(idx_now[:, b, :], idxT[:, bass.ds(bl * BLOCK, BLOCK)]).then_inc(s_idx, 1)

            with dve.If(flag == 1):
                stage_indices(0, 0, 0)
                dve.wait_ge(s_zero, STEPS - XB)
                for k in range(AHEAD):
                    make_hot(0, k, k)
                for l in range(2):
                    def add_in(bl, q, base):
                        g = l * GROUPS + bl * GB + q
                        dve.wait_ge(s_fold, START + g + 1)
                        dve.wait_ge(s_add, START + g)
                        cols = aggT[:, :, bass.ds(base, WIN)]
                        nc.vector.tensor_tensor(cols, cols, ps[:, 4 + q % 2, 0:KD * WIN].rearrange(
                            "p (k j) -> p k j", k=KD), ALU.add).then_inc(s_add, 1)

                    def ending(t, step):
                        end = t == TILES - 1
                        finish(l, l * TILES + t, t % 2, 2 if end else t % 2, 16 if end else 16 * (t // 2 + 1),
                               None if end else 16 * (t // 2), (step,))

                    def body(i, take=True, first=False, last=False):
                        base = []
                        for m in range(2):
                            bl = 2 * i + m
                            t = bl - LAG
                            n = l * TILES + t
                            base += nc.values_load_multi_w_load_instructions(
                                base_i[0:1, bass.ds(bl * GB, GB)], engines=(mybir.EngineType.DVE,),
                                min_val=0, max_val=N - 1,
                                skip_runtime_bounds_check_because="dst names nodes of the graph")[1]
                            for q in range(GB):
                                make_hot(l, bl * GB + q + AHEAD, (q + AHEAD) % GB)
                                k = m * GB + q - 2
                                if k >= 0:
                                    add_in(2 * i + k // GB, k % GB, base[k])
                                if q == 0:
                                    stage_indices(l, bl + 1, 1 - m)
                                if last and m:
                                    ending(*((TILES - 4, q + 1) if q < 3 else (TILES - 3, 1)))
                                elif take and q:
                                    finish(l, n, m, m, 16 * (i - LAG // 2 + 1),
                                           None if first else 16 * (i - LAG // 2), (q,))
                        add_in(2 * i + 1, GB - 2, base[2 * GB - 2])
                        if last:
                            ending(TILES - 3, 2)
                        add_in(2 * i + 1, GB - 1, base[2 * GB - 1])

                    with dve.Fori(0, LAG // 2) as i:
                        body(i, take=False)
                    body(LAG // 2, first=True)
                    with dve.Fori(LAG // 2 + 1, BLOCKS // 2 - 1) as i:
                        body(i)
                    body(BLOCKS // 2 - 1, last=True)
                    ending(TILES - 3, 3)
                    ending(TILES - 2, 1)
                    ending(TILES - 2, 2)
                    ending(TILES - 1, 1)
                    ending(TILES - 1, 2)
                    ending(TILES - 2, 3)
                    ending(TILES - 1, 3)
            with dve.Else():
                for b in range(XB):
                    dve.wait_ge(s_lnst[b], ln_stored_all(b))
                for l in range(2):
                    dve.wait_ge(g_zero, 3 * l + 3)
                    with dve.Fori(0, CHUNKS) as c:
                        n = l * CHUNKS + c
                        LINKED = 6

                        def then(ins, k):
                            ins.then_inc(g_link, 1)
                            dve.wait_ge(g_link, LINKED * n + k)

                        node, weight = dstT[:, bass.ds(c, 1)], wT[:, bass.ds(c, 1)]
                        nc.vector.tensor_copy(dst_b, node.to_broadcast([P, P])).then_inc(g_dstb, 1)
                        dve.wait_ge(g_row, n + 1)
                        then(nc.vector.tensor_scalar(eq, ps[:, 1, 0:P], node, None, ALU.is_equal), 1)
                        then(nc.vector.tensor_tensor(dst_b, eq, below, ALU.mult), 2)
                        nc.vector.tensor_reduce(col[:, 0:1], dst_b, AX.X, ALU.add)
                        then(nc.vector.tensor_scalar(col[:, 1:2], node, float(N), None, ALU.is_lt), 3)
                        nc.vector.tensor_tensor(col[:, 2:3], node, trash, ALU.subtract)
                        then(nc.vector.tensor_scalar(col[:, 3:4], col[:, 0:1], 0.0, col[:, 1:2],
                                                     ALU.is_equal, ALU.mult), 4)
                        then(nc.vector.tensor_tensor(col[:, 4:5], col[:, 2:3], col[:, 3:4], ALU.mult), 5)
                        then(nc.vector.tensor_tensor(gen_to, col[:, 4:5], trash, ALU.add), 6)
                        dve.wait_ge(g_rows, 16 * n + 16)
                        nc.vector.tensor_tensor(ht[:, 0, :], rows[:, 0, 0:D], rows[:, 0, D:2 * D], ALU.add)
                        nc.vector.tensor_scalar(eqw, eq, weight, None, ALU.mult).then_inc(g_eq, 1)
                        dve.wait_ge(g_sum, n + 1)
                        dve.wait_ge(g_sc, 16 * n + 16)

                    for t in range(2):
                        finish(l, l * TILES + t, t, t, 16, None)
                    with dve.Fori(1, TILES // 2) as j:
                        for b in range(2):
                            finish(l, l * TILES + 2 * j + b, b, b, 16 * (j + 1), 16 * j)
                    finish(l, l * TILES + TILES - 1, 0, 2, 16, None)


_INS = ["x", "src", "dst", "edge_weight", "L0_gnn_weight", "L1_gnn_W", "L1_gnn_b"]


def kernel(**inputs):
    import concourse.bacc as _bacc
    from concourse.bass_utils import run_bass_kernel_spmd as _run

    nc = _bacc.Bacc("TRN2", target_bir_lowering=False, num_devices=1)
    arrays, args = {}, []
    for name in _INS:
        a = np.ascontiguousarray(inputs[name])
        arrays[f"in_{name}_dram"] = a
        args.append(nc.dram_tensor(f"in_{name}_dram", a.shape, mybir.dt.from_np(a.dtype), kind="ExternalInput").ap())
    shape = tuple(inputs["x"].shape)
    args.append(nc.dram_tensor("out_0_dram", shape, mybir.dt.float32, kind="ExternalOutput").ap())
    gnn_kernel(nc, *args)
    r = _run(nc, [arrays], core_ids=[0])
    return r.results[0]["out_0_dram"]
```
